# Optimizing a Trainium2 kernel written in Bass

```python
import numpy as np
import jax
import jax.numpy as jnp

def _softmax(x, axis=-1):
    return jax.nn.softmax(x, axis=axis)

def _gelu(x):
    return jax.nn.gelu(x, approximate=True)

def _silu(x):
    return jax.nn.silu(x)

def _sigmoid(x):
    return jax.nn.sigmoid(x)

def _layernorm(x, axis=-1, eps=1e-05):
    m = jnp.mean(x, axis=axis, keepdims=True)
    v = jnp.var(x, axis=axis, keepdims=True)
    return (x - m) / jnp.sqrt(v + eps)

def _scatter_add(tgt, idx, src, axis=0):
    return tgt.at[idx].add(src)

def _segment_sum(src, seg, n):
    return jax.ops.segment_sum(src, seg, n)
kernel_name = 'mk_conv_seq_d2_conv_nchw512_r4_adc707'

def setup_inputs(seed: int=0):
    np.random.seed(seed)
    _w = jnp.asarray

    def _rec_inputs():
        import jax
        import jax.numpy as jnp
        _gk = jax.random.key(seed)
        x = -0.0003929 + 0.9999 * jax.random.normal(jax.random.fold_in(_gk, 1), (8, 128, 16, 16), jnp.float32)
        return x
    x = _rec_inputs()

    def _L0_conv_setup():
        import jax, jax.numpy as jnp
        import numpy as np
        UP = 2
        DOWN = 2
        NEG_SLOPE = 0.2
        MARGIN = 10
        FLRELU_SCALE = np.float32(2.0 ** 0.5)
        UP_PAD = ((10 + 1) // 2 + UP - 1, 10 // 2)
        DOWN_PAD = ((10 + 1) // 2, 10 // 2)
        _FILT = np.array([0.0, 0.00398, -0.01884, -0.05155, 0.12443, 0.44197, 0.44197, 0.12443, -0.05155, -0.01884, 0.00398, 0.0], dtype=np.float32)
        _FILT = _FILT / _FILT.sum()

        def _fir1d(x, k, up, down, pad0, pad1, axis):
            N, C, H, W = x.shape
            xr = x.reshape(N * C, 1, H, W)
            K = k.shape[0]
            kf = k[::-1].astype(x.dtype)
            if axis == 3:
                w = kf.reshape(1, 1, 1, K)
                lhs_dil = (1, up)
                strides = (1, down)
                padding = ((0, 0), (pad0, pad1 + up - 1))
            else:
                w = kf.reshape(1, 1, K, 1)
                lhs_dil = (up, 1)
                strides = (down, 1)
                padding = ((pad0, pad1 + up - 1), (0, 0))
            y = jax.lax.conv_general_dilated(xr, w, window_strides=strides, padding=padding, lhs_dilation=lhs_dil, dimension_numbers=('NCHW', 'OIHW', 'NCHW'))
            return y.reshape(N, C, y.shape[2], y.shape[3])

        def _sep_upfirdn(x, k, up, down, pad):
            x = _fir1d(x, k, up, down, pad[0], pad[1], axis=3)
            x = _fir1d(x, k, up, down, pad[0], pad[1], axis=2)
            return x
        key = jax.random.key(seed)
        k_in = jax.random.fold_in(key, 0)
        return {'input': jax.random.normal(k_in, (8, 128, 16, 16), dtype=jnp.float32), 'bias': jnp.zeros((128,), dtype=jnp.float32), 'up_filter': jnp.asarray(_FILT), 'down_filter': jnp.asarray(_FILT)}
    _L0_conv_all = _L0_conv_setup()
    _L0_conv_in = {k: v for k, v in _L0_conv_all.items() if k in ('bias', 'up_filter', 'down_filter')}
    del _L0_conv_all

    def _L1_conv_setup():
        import jax, jax.numpy as jnp
        import numpy as np
        import math
        C = 128
        HEADS = 8
        GROUPS = 32
        HIDDEN = C * 4
        EPS = 1e-05

        def group_norm(x, gamma, beta, groups, eps=EPS):
            b, c = (x.shape[0], x.shape[1])
            xg = x.reshape(b, groups, -1)
            mean = xg.mean(axis=-1, keepdims=True)
            var = xg.var(axis=-1, keepdims=True)
            xg = (xg - mean) * jax.lax.rsqrt(var + eps)
            xn = xg.reshape(x.shape)
            shape = (1, c) + (1,) * (x.ndim - 2)
            return xn * gamma.reshape(shape) + beta.reshape(shape)
        key = jax.random.key(seed)
        ks = jax.random.split(key, 10)
        s = lambda fan_in: 1.0 / math.sqrt(fan_in)
        inp = {'x': jax.random.normal(ks[0], (8, C, 32, 32), dtype=jnp.float32), 'gn1_gamma': jnp.ones((C,), jnp.float32), 'gn1_beta': jnp.zeros((C,), jnp.float32), 'qkv_w': jax.random.uniform(ks[1], (3 * C, C), jnp.float32, -s(C), s(C)), 'qkv_b': jax.random.uniform(ks[2], (3 * C,), jnp.float32, -s(C), s(C)), 'out_w': jax.random.uniform(ks[3], (C, C), jnp.float32, -s(C), s(C)), 'out_b': jax.random.uniform(ks[4], (C,), jnp.float32, -s(C), s(C)), 'gn2_gamma': jnp.ones((C,), jnp.float32), 'gn2_beta': jnp.zeros((C,), jnp.float32), 'mlp1_w': jax.random.uniform(ks[5], (2 * HIDDEN, C), jnp.float32, -s(C), s(C)), 'mlp2_w': jax.random.uniform(ks[6], (C, HIDDEN), jnp.float32, -s(HIDDEN), s(HIDDEN))}
        return inp
    _L1_conv_all = _L1_conv_setup()
    _L1_conv_in = {k: v for k, v in _L1_conv_all.items() if k in ('gn1_gamma', 'gn1_beta', 'qkv_w', 'qkv_b', 'out_w', 'out_b', 'gn2_gamma', 'gn2_beta', 'mlp1_w', 'mlp2_w')}
    del _L1_conv_all
    return {'x': x, 'L0_conv_bias': _L0_conv_in['bias'], 'L0_conv_up_filter': _L0_conv_in['up_filter'], 'L0_conv_down_filter': _L0_conv_in['down_filter'], 'L1_conv_gn1_gamma': _L1_conv_in['gn1_gamma'], 'L1_conv_gn1_beta': _L1_conv_in['gn1_beta'], 'L1_conv_qkv_w': _L1_conv_in['qkv_w'], 'L1_conv_qkv_b': _L1_conv_in['qkv_b'], 'L1_conv_out_w': _L1_conv_in['out_w'], 'L1_conv_out_b': _L1_conv_in['out_b'], 'L1_conv_gn2_gamma': _L1_conv_in['gn2_gamma'], 'L1_conv_gn2_beta': _L1_conv_in['gn2_beta'], 'L1_conv_mlp1_w': _L1_conv_in['mlp1_w'], 'L1_conv_mlp2_w': _L1_conv_in['mlp2_w']}

def reference(x, L0_conv_bias, L0_conv_up_filter, L0_conv_down_filter, L1_conv_gn1_gamma, L1_conv_gn1_beta, L1_conv_qkv_w, L1_conv_qkv_b, L1_conv_out_w, L1_conv_out_b, L1_conv_gn2_gamma, L1_conv_gn2_beta, L1_conv_mlp1_w, L1_conv_mlp2_w):
    import jax
    import jax.numpy as jnp

    def _L0_conv_ref(input, bias, up_filter, down_filter):
        import jax, jax.numpy as jnp
        import numpy as np
        UP = 2
        DOWN = 2
        NEG_SLOPE = 0.2
        MARGIN = 10
        FLRELU_SCALE = np.float32(2.0 ** 0.5)
        UP_PAD = ((10 + 1) // 2 + UP - 1, 10 // 2)
        DOWN_PAD = ((10 + 1) // 2, 10 // 2)
        _FILT = np.array([0.0, 0.00398, -0.01884, -0.05155, 0.12443, 0.44197, 0.44197, 0.12443, -0.05155, -0.01884, 0.00398, 0.0], dtype=np.float32)
        _FILT = _FILT / _FILT.sum()

        def _fir1d(x, k, up, down, pad0, pad1, axis):
            N, C, H, W = x.shape
            xr = x.reshape(N * C, 1, H, W)
            K = k.shape[0]
            kf = k[::-1].astype(x.dtype)
            if axis == 3:
                w = kf.reshape(1, 1, 1, K)
                lhs_dil = (1, up)
                strides = (1, down)
                padding = ((0, 0), (pad0, pad1 + up - 1))
            else:
                w = kf.reshape(1, 1, K, 1)
                lhs_dil = (up, 1)
                strides = (down, 1)
                padding = ((pad0, pad1 + up - 1), (0, 0))
            y = jax.lax.conv_general_dilated(xr, w, window_strides=strides, padding=padding, lhs_dilation=lhs_dil, dimension_numbers=('NCHW', 'OIHW', 'NCHW'))
            return y.reshape(N, C, y.shape[2], y.shape[3])

        def _sep_upfirdn(x, k, up, down, pad):
            x = _fir1d(x, k, up, down, pad[0], pad[1], axis=3)
            x = _fir1d(x, k, up, down, pad[0], pad[1], axis=2)
            return x
        out = input + bias[None, :, None, None]
        upf = up_filter * UP
        out = _sep_upfirdn(out, upf, UP, 1, UP_PAD)
        out = jax.nn.leaky_relu(out, NEG_SLOPE) * FLRELU_SCALE
        out = _sep_upfirdn(out, down_filter, 1, DOWN, DOWN_PAD)
        m = (MARGIN * UP - MARGIN * DOWN) // 2
        if m > 0:
            out = out[:, :, m:-m, m:-m]
        return out

    def _L1_conv_ref(x, gn1_gamma, gn1_beta, qkv_w, qkv_b, out_w, out_b, gn2_gamma, gn2_beta, mlp1_w, mlp2_w):
        import jax, jax.numpy as jnp
        import numpy as np
        import math
        C = 128
        HEADS = 8
        GROUPS = 32
        HIDDEN = C * 4
        EPS = 1e-05

        def group_norm(x, gamma, beta, groups, eps=EPS):
            b, c = (x.shape[0], x.shape[1])
            xg = x.reshape(b, groups, -1)
            mean = xg.mean(axis=-1, keepdims=True)
            var = xg.var(axis=-1, keepdims=True)
            xg = (xg - mean) * jax.lax.rsqrt(var + eps)
            xn = xg.reshape(x.shape)
            shape = (1, c) + (1,) * (x.ndim - 2)
            return xn * gamma.reshape(shape) + beta.reshape(shape)
        b, c, h, w = x.shape
        n = h * w
        head_dim = c // HEADS
        x_norm = group_norm(x, gn1_gamma, gn1_beta, GROUPS).reshape(b, c, n)
        qkv = jnp.einsum('oc,bcn->bon', qkv_w, x_norm) + qkv_b[None, :, None]
        q, k, v = jnp.split(qkv, 3, axis=1)
        split_heads = lambda t: t.reshape(b, HEADS, head_dim, n).transpose(0, 1, 3, 2)
        q, k, v = (split_heads(q), split_heads(k), split_heads(v))
        attn = jnp.einsum('bhnd,bhmd->bhnm', q, k) / math.sqrt(head_dim)
        attn = jax.nn.softmax(attn, axis=-1)
        x_attn = jnp.einsum('bhnm,bhmd->bhnd', attn, v)
        x_attn = x_attn.transpose(0, 1, 3, 2).reshape(b, c, n)
        x_attn = jnp.einsum('oc,bcn->bon', out_w, x_attn) + out_b[None, :, None]
        x_attn = group_norm(x_attn, gn2_gamma, gn2_beta, GROUPS)
        x_attn = x_attn.transpose(0, 2, 1)
        hgate = x_attn @ mlp1_w.T
        h1, gate = jnp.split(hgate, 2, axis=-1)
        x_attn = jax.nn.silu(h1) * gate
        x_attn = x_attn @ mlp2_w.T
        x_attn = x_attn.transpose(0, 2, 1).reshape(b, c, h, w)
        return x + x_attn

    def _gn(v, G=32, eps=1e-05):
        B_, C_, H_, W_ = v.shape
        g = v.reshape(B_, G, C_ // G, H_, W_)
        m = jnp.mean(g, axis=(2, 3, 4), keepdims=True)
        s = jnp.var(g, axis=(2, 3, 4), keepdims=True)
        return ((g - m) / jnp.sqrt(s + eps)).reshape(v.shape)

    def _ln_c(v, eps=1e-06):
        m = jnp.mean(v, axis=1, keepdims=True)
        s = jnp.var(v, axis=1, keepdims=True)
        return (v - m) / jnp.sqrt(s + eps)

    def _ln_t(v, eps=1e-05):
        m = jnp.mean(v, axis=-1, keepdims=True)
        s = jnp.var(v, axis=-1, keepdims=True)
        return (v - m) / jnp.sqrt(s + eps)

    def _to_tokens(v):
        B_, C_, H_, W_ = v.shape
        return v.reshape(B_, C_, H_ * W_).transpose(0, 2, 1)

    def _from_tokens(t, like):
        B_, C_, H_, W_ = like.shape
        return t.transpose(0, 2, 1).reshape(B_, C_, H_, W_)
    x = _L0_conv_ref(x, L0_conv_bias, L0_conv_up_filter, L0_conv_down_filter)
    x = _L1_conv_ref(x, L1_conv_gn1_gamma, L1_conv_gn1_beta, L1_conv_qkv_w, L1_conv_qkv_b, L1_conv_out_w, L1_conv_out_b, L1_conv_gn2_gamma, L1_conv_gn2_beta, L1_conv_mlp1_w, L1_conv_mlp2_w)
    return x

_drawn_inputs = setup_inputs


def setup_inputs(seed=0):
    import zlib

    import numpy as np

    out = dict(_drawn_inputs(seed))
    spreads = {'L0_conv_bias': (0.0, 0.1),
     'L1_conv_gn1_gamma': (1.0, 0.2),
     'L1_conv_gn1_beta': (0.0, 0.1),
     'L1_conv_gn2_gamma': (1.0, 0.2),
     'L1_conv_gn2_beta': (0.0, 0.428)}
    factors = {}
    for name, (base, spread) in spreads.items():
        noise = np.random.default_rng([zlib.crc32(name.encode()), seed]).standard_normal(out[name].shape)
        drawn = base * np.exp(spread * noise) if base else spread * noise
        out[name] = jnp.asarray(drawn.astype(out[name].dtype))
    for name, factor in factors.items():
        out[name] = (out[name] * factor).astype(out[name].dtype)
    return out
```

```python
from contextlib import ExitStack

import concourse.bass as bass
from concourse import mybir

F32 = mybir.dt.float32
F32R = mybir.dt.float32r
ALU = mybir.AluOpType
ACT = mybir.ActivationFunctionType
AX = mybir.AxisListType

B, C, W = 8, 128, 16
N = W * W
HEADS, D = 8, 16
HALF = HEADS // 2
HIDDEN = 4 * C
HC = HIDDEN // C
EPS = 1e-5
SLOPE = 0.2
GAIN = 1.4142135381698608
UPGAIN = 4.0
BH = B // 2 * C
CHUNKS = 8
WINDOW_ROWS = [0, 1, 3, 5, 7, 8]
WINDOW_OF = [0, 0, 1, 2, 3, 4, 5, 5]
UP_WEIGHT_OF = [0, 1, 2, 2, 2, 2, 3, 4]
UP_VARIANTS = 5
NWIN = len(WINDOW_ROWS)
ROW = 2 * 2 * D
RING = 3


def build(nc, xw, up_fast, up_slow, dn_fast, dn_slow, bias0, vecs, wqk, wv, bv, wo, w1, w2,
          ident, gmat, sel, out):
    ctx = ExitStack()
    with ctx:
        def sb(name, shape, dt=F32):
            return ctx.enter_context(nc.sbuf_tensor(name, shape, dt))

        def sem(name):
            return ctx.enter_context(nc.semaphore(name))

        ident_s = sb("ident_s", [128, 128])
        gmat_s = sb("gmat_s", [128, 128])
        sel_s = sb("sel_s", [128, HALF])
        fac = sb("fac", [128, 32 + 4 * UP_VARIANTS + 16 + 8])
        vec = sb("vec", [128, 8])
        g1w, g1b, g2w, g2b = (vec[:, j:j + 1] for j in range(4))
        bq, bk, bo = (vec[:, j:j + 1] for j in range(4, 7))
        bias_bc = sb("bias_bc", [128, C])
        bv_bc = sb("bv_bc", [128, C])
        up_w = sb("up_w", [128, UP_VARIANTS, 4, 32])
        dn_w = sb("dn_w", [128, 8, 16])
        wqk_s = sb("wqk_s", [128, 2 * C])
        wqk_hi = sb("wqk_hi", [128, 2 * C], F32R)
        wqk_lo = sb("wqk_lo", [128, 2 * C], F32R)
        wv_s = sb("wv_s", [128, C])
        wo_s = sb("wo_s", [128, 2, C])
        w1_s = sb("w1_s", [128, 2 * HIDDEN])
        w1_hi = sb("w1_hi", [128, 2 * HIDDEN], F32R)
        w1_lo = sb("w1_lo", [128, 2 * HIDDEN], F32R)
        w2_s = sb("w2_s", [128, HC * C])
        w2_hi = sb("w2_hi", [128, HC * C], F32R)
        w2_lo = sb("w2_lo", [128, HC * C], F32R)
        half_neg = sb("half_neg", [128, B])

        win = sb("win", [128, NWIN * B * C])
        up_t = sb("up_t", [128, CHUNKS * B * C])
        lrelu_neg = sb("lrelu_neg", [128, 2, BH])
        y = sb("y", [128, B, N])

        def win_at(t, half):
            a = (t * 2 + half) * BH
            return win[:, a:a + BH]

        def up_at(m, half):
            a = (m * 2 + half) * BH
            return up_t[:, a:a + BH]

        stat6 = sb("stat6", [128, B, 6])
        mv = sb("mv", [128, B, 2])
        sq = sb("sq", [128, B])
        gs = sb("gs", [128, B, 2])
        ve = sb("ve", [128, B])
        rstd = sb("rstd", [128, B])
        shift_t = sb("shift_t", [128, B])
        scale1 = sb("scale1", [128, B])
        shift1 = sb("shift1", [128, B])
        scale2 = sb("scale2", [128, B])
        shift2 = sb("shift2", [128, B])

        xn = win[:, 0:RING * N].rearrange("p (r n) -> p r n", r=RING)
        xn_hi = sb("xn_hi", [128, RING, N], F32R)
        xn_lo = sb("xn_lo", [128, RING, N], F32R)
        qk_parts = sb("qk_parts", [128, 2, 2, N], F32R)
        q_stack = [sb(f"q_stack{r}", [128, HEADS, N], F32R) for r in range(RING)]
        k_stack = [sb(f"k_stack{r}", [128, HEADS, N], F32R) for r in range(RING)]
        v_aug = sb("v_aug", [128, RING, 2, HEADS, 32])
        neg_max = sb("neg_max", [128, 2, 2, HALF])
        max_row = sb("max_row", [HALF, 2, N], F32R)
        probs = up_t[:, 0:2 * HALF * 2 * N].rearrange("p (u h c n) -> p u h c n", u=2, h=HALF, c=2)
        attn = up_t[:, 4096:4096 + B * N].rearrange("p (b n) -> p b n", b=B)
        sums = sb("sums", [128, 2, N])
        inv = sb("inv", [128, 2, 2, HALF])
        inv_wide = sb("inv_wide", [128, 2, 2, HALF, 32])
        weighted = sb("weighted", [128, 2, N])

        xm = up_t[:, 6144:6144 + B * N]
        xm_hi = sb("xm_hi", [128, B * N], F32R)
        xm_lo = sb("xm_lo", [128, B * N], F32R)
        silu_o = win[:, 1024:2048].rearrange("p (r n) -> p r n", r=2)
        gated = win[:, 2048:3072].rearrange("p (r n) -> p r n", r=2)
        gated_hi = sb("gated_hi", [128, 2, 512], F32R)
        gated_lo = sb("gated_lo", [128, 2, 512], F32R)
        result = win[:, 3072:3072 + B * N]

        def pb(name, banks):
            return ctx.enter_context(nc.psum_tensor(name, [128, banks, 512], F32))
        pm = pb("pm", 2)
        pt = [pb("pt0", 2), pb("pt1", 2)]
        po = pb("po", 1)
        px = pb("px", 1)
        up_bank = [pt[0][:, 0, :], pt[0][:, 1, :], pt[1][:, 0, :], pt[1][:, 1, :]]
        gn_bank = po[:, 0, 0:2 * B]

        fac_in = sem("fac_in")
        dn_in = sem("dn_in")
        bias_in = sem("bias_in")
        vec_in = sem("vec_in")
        const_in = sem("const_in")
        wqk_in = sem("wqk_in")
        w_in = sem("w_in")
        wmlp_in = sem("wmlp_in")
        win_in = [[sem(f"win_in{t}{h}") for h in range(2)] for t in range(NWIN)]
        kron_ready = sem("kron_ready")
        biased = [sem("biased_dve"), sem("biased_pool")]
        up_done = sem("up_done")
        neg_ready = sem("neg_ready")
        up_ready = sem("up_ready")
        down_done = sem("down_done")
        y_ready = sem("y_ready")
        bn_raw = sem("bn_raw")
        mean_ready = sem("mean_ready")
        gn_step = sem("gn_step")
        gn_done = sem("gn_done")
        gn_var = sem("gn_var")
        gn_rstd = sem("gn_rstd")
        gn_ready = sem("gn_ready")
        pool_step = sem("pool_step")
        wqk_split = sem("wqk_split")
        wmlp_split = sem("wmlp_split")
        stacks_clear = sem("stacks_clear")
        xn_made = sem("xn_made")
        xn_ready = sem("xn_ready")
        qk_done = sem("qk_done")
        qk_hi = sem("qk_hi")
        qk_lo = sem("qk_lo")
        stack_in = [sem(f"stack_in{r}") for r in range(RING)]
        v_done = sem("v_done")
        v_ready = sem("v_ready")
        max_done = sem("max_done")
        max_read = sem("max_read")
        row_in = [sem("row_in0"), sem("row_in1")]
        scores_done = sem("scores_done")
        probs_ready = sem("probs_ready")
        pv_done = sem("pv_done")
        sums_ready = sem("sums_ready")
        den_done = sem("den_done")
        inv_ready = sem("inv_ready")
        wide_ready = sem("wide_ready")
        inv_done = sem("inv_done")
        weighted_ready = sem("weighted_ready")
        proj_done = sem("proj_done")
        attn_ready = sem("attn_ready")
        xm_made = sem("xm_made")
        xm_ready = sem("xm_ready")
        h_done = sem("h_done")
        gate_done = sem("gate_done")
        silu_ready = sem("silu_ready")
        gated_made = sem("gated_made")
        gated_ready = sem("gated_ready")
        mlp_done = sem("mlp_done")
        result_ready = sem("result_ready")
        stored = sem("stored")

        GN_BATCHES = [(0, 4), (4, 8), (0, 6), (6, 8)]
        block = ctx.enter_context(nc.Block())

        @block.sync
        def _(sp):
            sp.dma_start(fac[:, 0:32], up_fast).then_inc(fac_in, 16)
            sp.dma_start(fac[:, 32:32 + 4 * UP_VARIANTS], up_slow).then_inc(fac_in, 16)
            sp.dma_start(bias_bc[:, :], bass.AP(tensor=bias0.tensor, offset=0, ap=[[0, 128], [1, C]])).then_inc(bias_in, 16)
            for half in range(2):
                for t in range(NWIN):
                    r0 = WINDOW_ROWS[t] * W
                    sp.dma_start(win_at(t, half), xw[r0:r0 + 128, half * BH:(half + 1) * BH]).then_inc(win_in[t][half], 16)
                if half == 0:
                    sp.dma_start(fac[:, 52:68], dn_fast).then_inc(dn_in, 16)
                    sp.dma_start(fac[:, 68:76], dn_slow).then_inc(dn_in, 16)
                    sp.dma_start(vec[:, :], vecs).then_inc(vec_in, 16)
            sp.dma_start(ident_s[:, :], ident).then_inc(const_in, 16)
            sp.dma_start(gmat_s[:, :], gmat).then_inc(const_in, 16)
            sp.dma_start(sel_s[:, :], sel).then_inc(const_in, 16)
            sp.dma_start(wqk_s[:, :], wqk).then_inc(wqk_in, 16)
            sp.dma_start(wv_s[:, :], wv).then_inc(w_in, 16)
            sp.dma_start(wo_s[:, :, :], wo).then_inc(w_in, 16)
            sp.dma_start(bv_bc[:, :], bass.AP(tensor=bv.tensor, offset=0, ap=[[0, 128], [1, C]])).then_inc(w_in, 16)
            sp.dma_start(w1_s[:, :], w1).then_inc(wmlp_in, 16)
            sp.dma_start(w2_s[:, :], w2).then_inc(wmlp_in, 16)

            def stack(i, k, first):
                sp.wait_ge(qk_hi, 2 * (i + 1))
                sp.wait_ge(qk_lo, 2 * (i + 1))
                if not first:
                    sp.wait_ge(scores_done, 4 * (i - 2))
                for j, (s, parts) in enumerate(((q_stack, (0, 1, 1, 0)), (k_stack, (0, 1, 0, 1)))):
                    for r, part in enumerate(parts):
                        sp.dma_start(s[k][r * D:(r + 1) * D, :, :].bitcast(F32),
                                     qk_parts[:, j, part, :].bitcast(F32)).then_inc(stack_in[k], 16)

            for i in range(RING):
                stack(i, i, True)
            for i in range(RING, B):
                stack(i, i % RING, False)
            for p in range(B // 2):
                sp.wait_ge(result_ready, p + 1)
                for b in (2 * p, 2 * p + 1):
                    sp.dma_start(out[b], result[:, b * N:(b + 1) * N]).then_inc(stored, 16)
            sp.wait_ge(stored, 16 * B)

        @block.gpsimd
        def _(pool):
            steps = 0

            def split(hi, lo, src):
                nonlocal steps
                pool.tensor_scalar(hi, src, 1.0, 0.0, ALU.mult, ALU.add).then_inc(pool_step, 1)
                steps += 1
                pool.wait_ge(pool_step, steps)
                return pool.tensor_tensor(lo, src, hi.bitcast(F32), ALU.subtract)

            pool.wait_ge(bias_in, 16)
            for t in range(NWIN):
                pool.wait_ge(win_in[t][1], 16)
                x4 = win_at(t, 1).rearrange("p (b c) -> p b c", c=C)
                pool.tensor_tensor(x4, x4, bias_bc[:, None, :].to_broadcast([128, B // 2, C]), ALU.add).then_inc(biased[1], 1)
            pool.memset(half_neg[:, :], -0.5).then_inc(stacks_clear, 1)
            fills = [(v_aug[:, :, :, :, :], 0.0), (v_aug[:, :, :, :, D:D + 1], 1.0)]
            for r in range(RING):
                fills += [(q_stack[r][ROW:128, :, :].bitcast(F32), 0.0), (k_stack[r][ROW:128, :, :].bitcast(F32), 0.0),
                          (k_stack[r][ROW:ROW + 1, :, :].bitcast(F32), 1.0)]
            for n, (tile, value) in enumerate(fills):
                pool.wait_ge(stacks_clear, n + 1)
                pool.memset(tile, value).then_inc(stacks_clear, 1)
            pool.wait_ge(stacks_clear, 3 + 3 * RING)
            pool.wait_ge(wqk_in, 16)
            split(wqk_hi[:, :], wqk_lo[:, :], wqk_s[:, :]).then_inc(wqk_split, 1)

            def rsqrt(n, b0, b1):
                pool.wait_ge(gn_var, n + 1)
                pool.tensor_tensor(rstd[:, b0:b1], ve[:, b0:b1], half_neg[:, b0:b1], ALU.pow).then_inc(gn_rstd, 1)

            def normalise(i, k):
                pool.tensor_scalar(xn[:, k, :], y[:, i, :], scale_of(scale1, i), scale_of(shift1, i),
                                   ALU.mult, ALU.add).then_inc(xn_made, 1)
                pool.wait_ge(xn_made, 2 * i + 1)
                pool.tensor_scalar(xn_hi[:, k, :], xn[:, k, :], 1.0, 0.0, ALU.mult, ALU.add).then_inc(xn_made, 1)
                pool.wait_ge(xn_made, 2 * i + 2)
                pool.tensor_tensor(xn_lo[:, k, :], xn[:, k, :], xn_hi[:, k, :].bitcast(F32), ALU.subtract).then_inc(xn_ready, 1)

            def scale_of(tile, i):
                return tile[:, bass.ds(i, 1)] if not isinstance(i, int) else tile[:, i:i + 1]

            def rows(i, k, half):
                pool.wait_ge(max_read, 10 * i + 5 * half + 5)
                pool.dma_start(q_stack[k][ROW:ROW + 1, half * HALF:(half + 1) * HALF, :].bitcast(F32),
                               max_row[:, half, :].bitcast(F32)).then_inc(row_in[half], 16)

            rsqrt(0, *GN_BATCHES[0])
            pool.wait_ge(gn_ready, 1)
            for i in range(2):
                normalise(i, i)
            rsqrt(1, *GN_BATCHES[1])
            normalise(2, 2)
            pool.wait_ge(wmlp_in, 32)
            split(w1_hi[:, :], w1_lo[:, :], w1_s[:, :]).then_inc(wmlp_split, 1)
            split(w2_hi[:, :], w2_lo[:, :], w2_s[:, :]).then_inc(wmlp_split, 1)
            rows(0, 0, 0)
            rows(0, 0, 1)
            pool.wait_ge(gn_ready, 2)

            def step(i, k, norm, maxima):
                if maxima:
                    rows(i + 1, (k + 1) % 3, 0)
                if norm:
                    pool.wait_ge(qk_done, i + 1)
                    pool.wait_ge(v_done, i + 1)
                    normalise(i + 3, k)
                if maxima:
                    rows(i + 1, (k + 1) % 3, 1)

            for i in range(B):
                step(i, i % 3, i + 3 < B, i + 1 < B)

            for n, (b0, b1) in enumerate(GN_BATCHES[2:]):
                rsqrt(2 + n, b0, b1)
                pool.wait_ge(gn_ready, 3 + n)
                for p in range(b0 // 2, b1 // 2):
                    for b in (2 * p, 2 * p + 1):
                        pool.tensor_scalar(xm[:, b * N:(b + 1) * N], attn[:, b, :], scale2[:, b:b + 1], shift2[:, b:b + 1],
                                           ALU.mult, ALU.add).then_inc(xm_made, 1)
                    pool.wait_ge(xm_made, 2 * p + 2)
                    cols = slice(2 * p * N, 2 * (p + 1) * N)
                    split(xm_hi[:, cols], xm_lo[:, cols], xm[:, cols]).then_inc(xm_ready, 1)

        @block.scalar
        def _(act):
            for n in range(2 * CHUNKS):
                act.wait_ge(up_done, n + 1)
                if n >= 2:
                    act.wait_ge(up_ready, n - 1)
                act.activation(lrelu_neg[:, n % 2, :], up_bank[n % 4], ACT.Copy,
                               scale=SLOPE * GAIN * UPGAIN).then_inc(neg_ready, 1)
            for b in range(B):
                act.wait_ge(down_done, b + 1)
                act.activation(y[:, b, :], pm[:, b % 2, 0:N], ACT.Copy).then_inc(y_ready, 1)

            act.wait_ge(vec_in, 16)

            def high_parts(i, k_prev, n_prev):
                act.wait_ge(qk_done, i + 1)
                if n_prev is not None:
                    act.wait_ge(stack_in[k_prev], n_prev)
                act.activation(qk_parts[:, 0, 0, :], px[:, 0, 0:N], ACT.Identity, bias=bq).then_inc(qk_hi, 1)
                act.activation(qk_parts[:, 1, 0, :], px[:, 0, N:2 * N], ACT.Identity, bias=bk).then_inc(qk_hi, 1)

            def exponentials(i, p, first):
                half = p // 2
                act.wait_ge(scores_done, 4 * i + p + 1)
                if not first:
                    act.wait_ge(pv_done, 2 * (i - 1) + half + 1)
                act.activation(probs[:, half, 2 * (p % 2):2 * (p % 2) + 2, :, :].rearrange("p h c n -> p (h c n)"),
                               pt[p % 2][:, :, :].rearrange("p a n -> p (a n)"), ACT.Exp, scale=D ** -0.5).then_inc(probs_ready, 1)

            def read_sums(i, first):
                act.wait_ge(pv_done, 2 * (i + 1))
                if not first:
                    act.wait_ge(weighted_ready, i)
                act.activation(sums[:, :, :].rearrange("p a n -> p (a n)"), po[:, 0, :], ACT.Copy).then_inc(sums_ready, 1)

            def read_proj(i):
                act.wait_ge(proj_done, i + 1)
                dst = attn[:, i, :] if isinstance(i, int) else attn[:, bass.ds(i, 1), :].rearrange("p a n -> p (a n)")
                act.activation(dst, px[:, 0, 0:N], ACT.Identity, bias=bo).then_inc(attn_ready, 1)

            def step(i, k, rounds, qkv, prev):
                exponentials(i, 0, not prev)
                if qkv:
                    high_parts(i + 2, (k + 1) % 3, 128 * (rounds + 1 + (k + 1) // 3))
                exponentials(i, 1, not prev)
                if prev:
                    read_sums(i - 1, i - 1 == 0 if isinstance(i, int) else False)
                exponentials(i, 2, not prev)
                exponentials(i, 3, not prev)
                if prev:
                    read_proj(i - 1)

            high_parts(0, 0, None)
            high_parts(1, 0, 128)
            for i in range(B):
                step(i, i % RING, i // RING, i + 2 < B, i >= 1)
            read_sums(B - 1, False)
            read_proj(B - 1)

            def silu(p, hc):
                n = HC * p + hc
                act.wait_ge(h_done, n + 1)
                if not (isinstance(n, int) and n < 2):
                    act.wait_ge(gated_made, 2 * (n - 1))
                act.activation(silu_o[:, hc % 2, :], pm[:, hc % 2, :], ACT.Silu).then_inc(silu_ready, 1)

            for hc in range(HC):
                silu(0, hc)
            with act.Fori(1, B // 2) as p:
                for hc in range(HC):
                    silu(p, hc)

        @block.tensor
        def _(pe):
            def three(dst, w_hi, w_lo, x_hi, x_lo, start, stop):
                pe.matmul(dst, w_hi, x_hi, start=start, stop=False)
                pe.matmul(dst, w_hi, x_lo, start=False, stop=False)
                return pe.matmul(dst, w_lo, x_hi, start=False, stop=stop)

            pe.wait_ge(kron_ready, 1)
            for half in range(2):
                for m in range(CHUNKS):
                    n = half * CHUNKS + m
                    if n == 1:
                        pe.wait_ge(kron_ready, 2)
                    pe.wait_ge(biased[half], WINDOW_OF[m] + 1)
                    if n >= 4:
                        pe.wait_ge(up_ready, n - 3)
                    pe.matmul(up_bank[n % 4], up_w[:, UP_WEIGHT_OF[m], :, :].rearrange("p a b -> p (a b)"),
                              win_at(WINDOW_OF[m], half), start=True, stop=True).then_inc(up_done, 1)

            def group_means(n):
                b0, b1 = GN_BATCHES[n]
                pe.wait_ge(mean_ready, n + 1)
                pe.matmul(gn_bank[:, 0:2 * (b1 - b0)], gmat_s[:, :], mv[:, b0:b1, :].rearrange("p b s -> p (b s)"),
                          start=True, stop=True).then_inc(gn_done, 1)

            pe.wait_ge(kron_ready, 3)
            for b in range(B):
                half = b // (B // 2)
                if b % (B // 2) == 0:
                    pe.wait_ge(up_ready, CHUNKS * (half + 1))
                if b >= 2:
                    pe.wait_ge(y_ready, b - 1)
                for m in range(CHUNKS):
                    o0, o1 = max(0, 2 * m - 3), min(W, 2 * m + 5)
                    col = (b % (B // 2)) * C
                    mm = pe.matmul(pm[:, b % 2, o0 * W:o1 * W], up_at(m, half)[:, col:col + C],
                                   dn_w[:, o0 - 2 * m + 3:o1 - 2 * m + 3, :].rearrange("p a b -> p (a b)"),
                                   start=(m == 0), stop=(m == CHUNKS - 1), skip_group_check=True)
                mm.then_inc(down_done, 1)
                if b == 4:
                    pe.wait_ge(const_in, 48)
                    group_means(0)

            def project_qk(i, k, first):
                pe.wait_ge(xn_ready, i + 1)
                if not first:
                    pe.wait_ge(v_ready, i)
                    if not (isinstance(i, int) and i < 4):
                        pe.wait_ge(attn_ready, i - 3)
                for j in range(2):
                    mm = three(px[:, 0, j * N:(j + 1) * N], wqk_hi[:, j * C:(j + 1) * C], wqk_lo[:, j * C:(j + 1) * C],
                               xn_hi[:, k, :], xn_lo[:, k, :], True, True)
                mm.then_inc(qk_done, 1)

            def project_v(i, k):
                pe.wait_ge(qk_lo, 2 * (i + 1))
                for c in range(2):
                    mm = pe.matmul(px[:, 0, c * C:(c + 1) * C], xn[:, k, c * 128:(c + 1) * 128], wv_s[:, :],
                                   start=True, stop=True)
                mm.then_inc(v_done, 1)

            def maxima(i, k, rounds, h):
                e = 10 * i + 5 * (h // HALF) + h % HALF
                bank = (5 * (h // HALF) + h % HALF) % 2
                if h == 0:
                    pe.wait_ge(stack_in[k], 128 * (rounds + 1))
                if not (isinstance(e, int) and e < 2):
                    pe.wait_ge(max_read, e - 1)
                for c in range(2):
                    mm = pe.matmul(pm[:, bank, c * N:(c + 1) * N], q_stack[k][:, h, c * 128:(c + 1) * 128],
                                   k_stack[k][:, h, :], start=True, stop=True)
                mm.then_inc(max_done, 1)

            def turn_maxima(i, half):
                e = 10 * i + 5 * half + 4
                pe.wait_ge(max_read, e)
                for c in range(2):
                    mm = pe.transpose(pm[0:HALF, (5 * half + 4) % 2, c * 128:(c + 1) * 128], neg_max[:, half, c, :], ident_s[:, :])
                mm.then_inc(max_done, 1)

            def scores(i, k, p):
                if p % 2 == 0:
                    pe.wait_ge(row_in[p // 2], 16 * (i + 1))
                if not (isinstance(i, int) and 4 * i + p < 2):
                    pe.wait_ge(probs_ready, 4 * i + p - 1)
                for a in range(2):
                    h = 2 * p + a
                    for c in range(2):
                        mm = pe.matmul(pt[p % 2][:, a, c * N:(c + 1) * N], k_stack[k][:, h, c * 128:(c + 1) * 128],
                                       q_stack[k][:, h, :], start=True, stop=True)
                mm.then_inc(scores_done, 1)

            def weigh(i, k, half, first):
                pe.wait_ge(probs_ready, 4 * i + 2 * half + 2)
                pe.wait_ge(v_ready, i + 1)
                if half == 0 and not first:
                    pe.wait_ge(sums_ready, i)
                for c in range(2):
                    for g in range(HALF):
                        mm = pe.matmul(po[32 * g:32 * g + 32, 0, half * N:(half + 1) * N],
                                       v_aug[:, k, c, half * HALF + g, :], probs[:, half, g, c, :],
                                       start=(c == 0), stop=(c == 1), skip_group_check=True)
                mm.then_inc(pv_done, 1)

            def turn_sums(i):
                pe.wait_ge(sums_ready, i + 1)
                for c in range(2):
                    for half in range(2):
                        a = 2 * C + (2 * c + half) * HALF
                        mm = pe.matmul(px[:, 0, a:a + HALF], sums[:, half, c * 128:(c + 1) * 128], sel_s[:, :],
                                       start=True, stop=True)
                mm.then_inc(den_done, 1)

            def turn_inverse(i):
                pe.wait_ge(wide_ready, i + 1)
                for half in range(2):
                    for c in range(2):
                        mm = pe.transpose(px[:, 0, half * N + c * 128:half * N + (c + 1) * 128],
                                          inv_wide[:, c, half, :, :].rearrange("p g d -> p (g d)"), ident_s[:, :])
                mm.then_inc(inv_done, 1)

            def project_out(i):
                pe.wait_ge(weighted_ready, i + 1)
                for half in range(2):
                    mm = pe.matmul(px[:, 0, 0:N], wo_s[:, half, :], weighted[:, half, :], start=(half == 0), stop=(half == 1))
                mm.then_inc(proj_done, 1)

            def step(i, k, rounds, qkv, nxt, prev):
                kn = (k + 1) % 3
                rn = rounds + (k + 1) // 3
                if nxt:
                    maxima(i + 1, kn, rn, 0)
                    maxima(i + 1, kn, rn, 1)
                scores(i, k, 0)
                if qkv:
                    project_qk(i + 2, (k + 2) % 3, False)
                if nxt:
                    maxima(i + 1, kn, rn, 2)
                    maxima(i + 1, kn, rn, 3)
                scores(i, k, 1)
                if prev:
                    weigh(i - 1, (k + 2) % 3, 1, False)
                if nxt:
                    turn_maxima(i + 1, 0)
                    maxima(i + 1, kn, rn, 4)
                    maxima(i + 1, kn, rn, 5)
                if qkv:
                    project_v(i + 2, (k + 2) % 3)
                if prev:
                    if not qkv:
                        pe.wait_ge(attn_ready, i - 1)
                    turn_sums(i - 1)
                scores(i, k, 2)
                if nxt:
                    maxima(i + 1, kn, rn, 6)
                    maxima(i + 1, kn, rn, 7)
                if prev:
                    turn_inverse(i - 1)
                scores(i, k, 3)
                weigh(i, k, 0, not prev)
                if prev:
                    project_out(i - 1)
                if nxt:
                    turn_maxima(i + 1, 1)

            pe.wait_ge(wqk_split, 1)
            pe.wait_ge(w_in, 48)
            pe.wait_ge(stacks_clear, 3 + 3 * RING)
            project_qk(0, 0, True)
            project_v(0, 0)
            project_qk(1, 1, False)
            project_v(1, 1)
            group_means(1)
            pe.wait_ge(y_ready, B)
            for h in range(HEADS):
                maxima(0, 0, 0, h)
                if h % HALF == HALF - 1:
                    turn_maxima(0, h // HALF)
            pe.wait_ge(gn_step, GN_READS[1])
            for i in range(B):
                step(i, i % RING, i // RING, i + 2 < B, i + 1 < B, i >= 1)
            weigh(7, 1, 1, False)
            pe.wait_ge(attn_ready, B - 1)
            turn_sums(7)
            group_means(2)
            turn_inverse(7)
            project_out(7)
            pe.wait_ge(gn_step, GN_READS[2])
            group_means(3)

            def up_project(p, hc, first):
                n = HC * p + hc
                if hc == 0:
                    pe.wait_ge(xm_ready, p + 1)
                if not (first and hc < 2):
                    pe.wait_ge(silu_ready, n - 1)
                cols = slice(2 * p * N, 2 * (p + 1) * N) if isinstance(p, int) else bass.ds(p * 2 * N, 2 * N)
                mm = three(pm[:, hc % 2, :], w1_hi[:, hc * C:(hc + 1) * C], w1_lo[:, hc * C:(hc + 1) * C],
                           xm_hi[:, cols], xm_lo[:, cols], True, True)
                mm.then_inc(h_done, 1)
                if not (first and hc < 2):
                    pe.wait_ge(gated_made, 2 * (n - 1) - 1)
                g = HIDDEN + hc * C
                mm = three(pt[0][:, hc % 2, :], w1_hi[:, g:g + C], w1_lo[:, g:g + C],
                           xm_hi[:, cols], xm_lo[:, cols], True, True)
                mm.then_inc(gate_done, 1)

            def down_project(p, hc):
                n = HC * p + hc
                pe.wait_ge(gated_ready, n + 1)
                if hc == 0 and not (isinstance(p, int) and p == 0):
                    pe.wait_ge(result_ready, p)
                three(pt[1][:, 0, :], w2_hi[:, hc * C:(hc + 1) * C], w2_lo[:, hc * C:(hc + 1) * C],
                      gated_hi[:, hc % 2, :], gated_lo[:, hc % 2, :], hc == 0, hc == HC - 1).then_inc(mlp_done, 1)

            pe.wait_ge(wmlp_split, 2)
            pe.wait_ge(max_read, 10 * B)
            pe.wait_ge(probs_ready, 4 * B)
            for hc in range(HC):
                up_project(0, hc, True)
                if hc >= 2:
                    down_project(0, hc - 2)
            with pe.Fori(1, B // 2) as p:
                for hc in range(HC):
                    up_project(p, hc, False)
                    if hc < 2:
                        down_project(p - 1, hc + 2)
                    else:
                        down_project(p, hc - 2)
            for hc in (2, 3):
                down_project(B // 2 - 1, hc)

        @block.vector
        def _(dve):
            steps = 0

            def chain(ins):
                nonlocal steps
                steps += 1
                ins.then_inc(gn_step, 1)
                dve.wait_ge(gn_step, steps)

            fast = fac[:, 0:32]
            slow = fac[:, 32:52].rearrange("p (v a) -> p v a", v=UP_VARIANTS)
            dve.wait_ge(fac_in, 32)
            for v in range(UP_VARIANTS):
                ins = dve.tensor_tensor(up_w[:, v, :, :], slow[:, v, :, None].to_broadcast([128, 4, 32]),
                                        fast[:, None, :].to_broadcast([128, 4, 32]), ALU.mult)
                if v in (0, UP_VARIANTS - 1):
                    ins.then_inc(kron_ready, 1)
            dve.wait_ge(bias_in, 16)
            for t in range(NWIN):
                dve.wait_ge(win_in[t][0], 16)
                x4 = win_at(t, 0).rearrange("p (b c) -> p b c", c=C)
                dve.tensor_tensor(x4, x4, bias_bc[:, None, :].to_broadcast([128, B // 2, C]), ALU.add).then_inc(biased[0], 1)
            dve.wait_ge(dn_in, 32)
            dve.tensor_tensor(dn_w[:, :, :], fac[:, 68:76, None].to_broadcast([128, 8, 16]),
                              fac[:, None, 52:68].to_broadcast([128, 8, 16]), ALU.mult).then_inc(kron_ready, 1)
            for n in range(2 * CHUNKS):
                dve.wait_ge(neg_ready, n + 1)
                dve.scalar_tensor_tensor(out=up_at(n % CHUNKS, n // CHUNKS), in0=up_bank[n % 4], scalar=GAIN * UPGAIN,
                                         in1=lrelu_neg[:, n % 2, :], op0=ALU.mult, op1=ALU.max).then_inc(up_ready, 1)

            def coefficients(n, gamma, beta, scale, shift):
                b0, b1 = GN_BATCHES[n]
                s = slice(b0, b1)
                chain(dve.tensor_tensor(sq[:, s], mv[:, s, 0], mv[:, s, 0], ALU.mult))
                dve.tensor_tensor(mv[:, s, 1], mv[:, s, 1], sq[:, s], ALU.add).then_inc(mean_ready, 1)
                dve.wait_ge(gn_done, n + 1)
                chain(dve.tensor_copy(gs[:, s, :], gn_bank[:, 0:2 * (b1 - b0)].rearrange("p (b s) -> p b s", s=2)))
                assert steps == GN_READS[n]
                chain(dve.tensor_tensor(sq[:, s], gs[:, s, 0], gs[:, s, 0], ALU.mult))
                chain(dve.tensor_tensor(sq[:, s], gs[:, s, 1], sq[:, s], ALU.subtract))
                dve.tensor_scalar(ve[:, s], sq[:, s], EPS, None, ALU.add).then_inc(gn_var, 1)
                dve.wait_ge(gn_rstd, n + 1)
                chain(dve.tensor_scalar(scale[:, s], rstd[:, s], gamma, None, ALU.mult))
                chain(dve.tensor_tensor(shift_t[:, s], gs[:, s, 0], scale[:, s], ALU.mult))
                dve.tensor_scalar(shift[:, s], shift_t[:, s], -1.0, beta, ALU.mult, ALU.add).then_inc(gn_ready, 1)

            dve.wait_ge(vec_in, 16)
            for half in range(2):
                for b in range(4 * half, 4 * half + 4):
                    dve.wait_ge(y_ready, b + 1)
                    chain(dve.bn_stats(stat6[:, b, :], y[:, b, :]))
                    chain(dve.bn_aggr(mv[:, b, :], stat6[:, b, :]))
                if half == 0:
                    coefficients(0, g1w, g1b, scale1, shift1)

            def low_parts(i):
                dve.wait_ge(qk_hi, 2 * (i + 1))
                for j, bias in enumerate((bq, bk)):
                    dve.scalar_tensor_tensor(out=qk_parts[:, j, 1, :], in0=px[:, 0, j * N:(j + 1) * N], scalar=bias,
                                             in1=qk_parts[:, j, 0, :].bitcast(F32), op0=ALU.add,
                                             op1=ALU.subtract).then_inc(qk_lo, 1)

            def read_v(i, k, first):
                dve.wait_ge(v_done, i + 1)
                if not first:
                    dve.wait_ge(den_done, i - 2)
                for c in range(2):
                    ins = dve.tensor_tensor(v_aug[:, k, c, :, 0:D], px[:, 0, c * C:(c + 1) * C].rearrange("p (h d) -> p h d", d=D),
                                            bv_bc[:, :].rearrange("p (h d) -> p h d", d=D), ALU.add)
                ins.then_inc(v_ready, 1)

            def reduce_max(i, h, first):
                e = 10 * i + 5 * (h // HALF) + h % HALF
                dve.wait_ge(max_done, e + 1)
                bank = (5 * (h // HALF) + h % HALF) % 2
                dve.tensor_reduce(neg_max[:, h // HALF, :, h % HALF], pm[:, bank, :].rearrange("p (c n) -> p c n", c=2),
                                  AX.X, ALU.max, negate=True).then_inc(max_read, 1)

            def read_rows(i, half, first):
                dve.wait_ge(max_done, 10 * i + 5 * half + 5)
                if not first:
                    dve.wait_ge(row_in[half], 16 * i)
                dve.tensor_copy(max_row[:, half, :], pm[0:HALF, (5 * half + 4) % 2, 0:N]).then_inc(max_read, 1)

            def invert(i, first):
                dve.wait_ge(den_done, i + 1)
                dve.reciprocal(inv[:, :, :, :].rearrange("p c a g -> p (c a g)"),
                               px[:, 0, 2 * C:2 * C + 4 * HALF]).then_inc(inv_ready, 1)
                dve.wait_ge(inv_ready, i + 1)
                if not first:
                    dve.wait_ge(inv_done, i)
                dve.tensor_copy(inv_wide[:, :, :, :, :].rearrange("p c a g d -> p (c a g) d"),
                                inv[:, :, :, :].rearrange("p c a g -> p (c a g)")[:, :, None].to_broadcast([128, 4 * HALF, 32])
                                ).then_inc(wide_ready, 1)

            def normalise(i, first):
                dve.wait_ge(inv_done, i + 1)
                if not first:
                    dve.wait_ge(proj_done, i)
                dve.tensor_tensor(weighted[:, :, :].rearrange("p a n -> p (a n)"), px[:, 0, :],
                                  sums[:, :, :].rearrange("p a n -> p (a n)"), ALU.mult).then_inc(weighted_ready, 1)

            def statistics(i):
                ii = slice(i, i + 1) if isinstance(i, int) else bass.ds(i, 1)
                dve.wait_ge(attn_ready, i + 1)
                dve.bn_stats(stat6[:, ii, :].rearrange("p a s -> p (a s)"), attn[:, ii, :].rearrange("p a n -> p (a n)")).then_inc(bn_raw, 1)
                dve.wait_ge(bn_raw, 2 * i + 1)
                dve.bn_aggr(mv[:, ii, :].rearrange("p a s -> p (a s)"), stat6[:, ii, :].rearrange("p a s -> p (a s)")).then_inc(bn_raw, 1)

            def step(i, k, qkv, nxt, prev, prev2):
                if nxt:
                    reduce_max(i + 1, 0, False)
                    reduce_max(i + 1, 1, False)
                if qkv:
                    low_parts(i + 2)
                if nxt:
                    reduce_max(i + 1, 2, False)
                    reduce_max(i + 1, 3, False)
                    read_rows(i + 1, 0, False)
                    reduce_max(i + 1, 4, False)
                    reduce_max(i + 1, 5, False)
                if qkv:
                    read_v(i + 2, (k + 2) % 3, isinstance(i, int) and i + 2 < 3)
                if prev:
                    invert(i - 1, isinstance(i, int) and i == 1)
                if nxt:
                    reduce_max(i + 1, 6, False)
                    reduce_max(i + 1, 7, False)
                if prev:
                    normalise(i - 1, isinstance(i, int) and i == 1)
                if prev2:
                    statistics(i - 2)
                if nxt:
                    read_rows(i + 1, 1, False)

            dve.wait_ge(w_in, 48)
            dve.wait_ge(stacks_clear, 3 + 3 * RING)
            for i in range(2):
                low_parts(i)
                read_v(i, i, True)
            coefficients(1, g1w, g1b, scale1, shift1)
            for half in range(2):
                for h in range(half * HALF, (half + 1) * HALF):
                    reduce_max(0, h, True)
                read_rows(0, half, True)
            for i in range(B):
                step(i, i % RING, i + 2 < B, i + 1 < B, i >= 1, i >= 2)
            invert(7, False)
            dve.wait_ge(bn_raw, 2 * 6)
            coefficients(2, g2w, g2b, scale2, shift2)
            normalise(7, False)
            statistics(6)
            statistics(7)
            dve.wait_ge(bn_raw, 2 * B)
            coefficients(3, g2w, g2b, scale2, shift2)

            def gate(p, hc, first):
                n = HC * p + hc
                dve.wait_ge(silu_ready, n + 1)
                dve.wait_ge(gate_done, n + 1)
                dve.tensor_tensor(gated[:, hc % 2, :], pt[0][:, hc % 2, :], silu_o[:, hc % 2, :], ALU.mult).then_inc(gated_made, 1)
                dve.wait_ge(gated_made, 2 * n + 1)
                if not (first and hc < 2):
                    dve.wait_ge(mlp_done, n - 1)
                dve.tensor_copy(gated_hi[:, hc % 2, :], gated[:, hc % 2, :]).then_inc(gated_made, 1)
                dve.wait_ge(gated_made, 2 * n + 2)
                dve.tensor_tensor(gated_lo[:, hc % 2, :], gated[:, hc % 2, :], gated_hi[:, hc % 2, :].bitcast(F32),
                                  ALU.subtract).then_inc(gated_ready, 1)

            def residual(p):
                dve.wait_ge(mlp_done, HC * (p + 1))
                cols = slice(2 * p * N, 2 * (p + 1) * N) if isinstance(p, int) else bass.ds(p * 2 * N, 2 * N)
                dve.tensor_tensor(result[:, cols], pt[1][:, 0, :], y[:, :, :].rearrange("p b n -> p (b n)")[:, cols],
                                  ALU.add).then_inc(result_ready, 1)

            for hc in range(HC):
                gate(0, hc, True)
            with dve.Fori(1, B // 2) as p:
                for hc in range(HC):
                    gate(p, hc, False)
                    if hc == 1:
                        residual(p - 1)
            residual(B // 2 - 1)


GN_READS = [10, 24, 30, 36]


def kernel(x, L0_conv_bias, L0_conv_up_filter, L0_conv_down_filter, L1_conv_gn1_gamma, L1_conv_gn1_beta,
           L1_conv_qkv_w, L1_conv_qkv_b, L1_conv_out_w, L1_conv_out_b, L1_conv_gn2_gamma, L1_conv_gn2_beta,
           L1_conv_mlp1_w, L1_conv_mlp2_w):
    import numpy as np
    import concourse.bacc as bacc
    from concourse.bass_utils import run_bass_kernel_spmd

    a = np.asarray

    def shifted(filt, rows, cols, tap):
        filt = a(filt)
        table = np.zeros((rows, cols), filt.dtype)
        for j in range(rows):
            for i in range(cols):
                if 0 <= tap(i, j) < filt.shape[0]:
                    table[j, i] = filt[tap(i, j)]
        return table

    up, down = L0_conv_up_filter, L0_conv_down_filter
    up_fast = np.tile(shifted(up, 16, 32, lambda i, j: 5 + i - 2 * j), (8, 1))
    slow = [shifted(up, 8, 4, lambda i, j, s=s: s + i - 2 * j) for s in (5, 9, 11, 13, 17)]
    up_slow = np.repeat(np.concatenate(slow, axis=1), 16, axis=0)
    dn_fast = np.tile(shifted(down, 32, 16, lambda o, r: 6 + 2 * o - r), (4, 1))
    dn_slow = np.repeat(shifted(down, 4, 8, lambda o, r: 2 * o - r), 32, axis=0)

    order = np.arange(C).reshape(HEADS, D).T.ravel()
    w, b = a(L1_conv_qkv_w), a(L1_conv_qkv_b)
    wqk = np.concatenate([w[0:C][order], w[C:2 * C][order]], axis=0).T
    wo = np.zeros((128, 2, C), w.dtype)
    for h in range(HEADS):
        wo[32 * (h % HALF):32 * (h % HALF) + D, h // HALF, :] = a(L1_conv_out_w)[:, h * D:(h + 1) * D].T
    vecs = np.zeros((128, 8), w.dtype)
    for j, v in enumerate((L1_conv_gn1_gamma, L1_conv_gn1_beta, L1_conv_gn2_gamma, L1_conv_gn2_beta,
                           b[0:C][order], b[C:2 * C][order], L1_conv_out_b)):
        vecs[:, j] = a(v)
    sel = np.zeros((128, HALF), np.float32)
    for g in range(HALF):
        sel[32 * g + D, g] = 1.0
    arrays = {
        "xw": a(x).transpose(2, 3, 0, 1).reshape(N, B * C),
        "up_fast": up_fast, "up_slow": up_slow, "dn_fast": dn_fast, "dn_slow": dn_slow,
        "bias0": a(L0_conv_bias), "vecs": vecs, "wqk": wqk, "wv": w[2 * C:].T, "bv": b[2 * C:],
        "wo": wo, "w1": a(L1_conv_mlp1_w).T,
        "w2": a(L1_conv_mlp2_w).T.reshape(HC, C, C).transpose(1, 0, 2).reshape(C, HC * C),
        "ident": np.eye(128, dtype=np.float32),
        "gmat": np.kron(np.eye(32, dtype=np.float32), np.full((4, 4), 0.25, np.float32)),
        "sel": sel,
    }
    arrays = {f"in_{k}": np.ascontiguousarray(v) for k, v in arrays.items()}
    nc = bacc.Bacc("TRN2", target_bir_lowering=False, num_devices=1)
    ins = [nc.dram_tensor(k, v.shape, mybir.dt.from_np(v.dtype), kind="ExternalInput").ap() for k, v in arrays.items()]
    out = nc.dram_tensor("out", (B, C, N), F32, kind="ExternalOutput").ap()
    build(nc, *ins, out)
    r = run_bass_kernel_spmd(nc, [arrays], core_ids=[0])
    return r.results[0]["out"].reshape(B, C, W, W)
```

```python
from contextlib import ExitStack

import concourse.bass as bass
from concourse import mybir

F32 = mybir.dt.float32
F32R = mybir.dt.float32r
ALU = mybir.AluOpType
ACT = mybir.ActivationFunctionType
AX = mybir.AxisListType

B, C, W = 8, 128, 16
N = W * W
HEADS, D = 8, 16
HALF = HEADS // 2
HIDDEN = 4 * C
HC = HIDDEN // C
EPS = 1e-5
SLOPE = 0.2
GAIN = 1.4142135381698608
UPGAIN = 4.0
BH = B // 2 * C
CHUNKS = 8
WINDOW_ROWS = [0, 1, 3, 5, 7, 8]
WINDOW_OF = [0, 0, 1, 2, 3, 4, 5, 5]
UP_WEIGHT_OF = [0, 1, 2, 2, 2, 2, 3, 4]
UP_VARIANTS = 5
NWIN = len(WINDOW_ROWS)
DVE_WINDOWS = [(0, 0), (1, 0), (2, 0), (4, 0)]
POOL_WINDOWS = [(3, 0), (5, 0)] + [(t, 1) for t in range(NWIN)]
ROW = 64
RING = 3
MAX_BANK = [0, 1, 0, 1, 0, 0, 1, 0]
STACKED = 3
MLP_RING = 4
MLP_LAG = 4
GN1_BATCHES = [(0, 1), (1, 4), (4, 8)]
GN2_BATCHES = [(0, 2), (2, 4), (4, 6), (6, 7), (7, 8)]
GN_BATCHES = GN1_BATCHES + GN2_BATCHES


def build(nc, xw, factors, bias0, vecs, wqk, wv, bv, wo, w1, w2,
          ident, gmat, out):
    ctx = ExitStack()
    with ctx:
        def sb(name, shape, dt=F32):
            return ctx.enter_context(nc.sbuf_tensor(name, shape, dt))

        def sem(name):
            return ctx.enter_context(nc.semaphore(name))

        ident_s = sb("ident_s", [128, 128])
        gmat_s = sb("gmat_s", [128, 128])
        fac = sb("fac", [128, 32 + 4 * UP_VARIANTS + 16 + 8])
        vec = sb("vec", [128, 8])
        g1w, g1b, g2w, g2b = (vec[:, j:j + 1] for j in range(4))
        bq, bk, bo = (vec[:, j:j + 1] for j in range(4, 7))
        bias_bc = sb("bias_bc", [128, C])
        bv_bc = sb("bv_bc", [128, C])
        up_w = sb("up_w", [128, UP_VARIANTS, 4, 32])
        dn_w = sb("dn_w", [128, 8, 16])
        wqk_s = sb("wqk_s", [128, 2 * C])
        wqk_hi = sb("wqk_hi", [128, 2 * C], F32R)
        wqk_lo = sb("wqk_lo", [128, 2 * C], F32R)
        wv_s = sb("wv_s", [128, C])
        wo_s = sb("wo_s", [128, 2, C])
        w1_s = sb("w1_s", [128, 2 * HIDDEN])
        w1_hi = sb("w1_hi", [128, 2 * HIDDEN], F32R)
        w1_lo = sb("w1_lo", [128, 2 * HIDDEN], F32R)
        w2_s = sb("w2_s", [128, HC * C])
        w2_hi = sb("w2_hi", [128, HC * C], F32R)
        w2_lo = sb("w2_lo", [128, HC * C], F32R)
        half_neg = sb("half_neg", [128, B])
        rest = sb("rest", [128, 2])

        win = sb("win", [128, NWIN * B * C])
        up_t = sb("up_t", [128, CHUNKS * B * C])
        lrelu_neg = sb("lrelu_neg", [128, 2, BH])
        y = sb("y", [128, B, N])

        def win_at(t, half):
            a = (t * 2 + half) * BH
            return win[:, a:a + BH]

        def up_at(m, half):
            a = (m * 2 + half) * BH
            return up_t[:, a:a + BH]

        stat6 = sb("stat6", [128, B, 6])
        mv = sb("mv", [128, B, 2])
        sq = sb("sq", [128, B])
        gs = sb("gs", [128, B, 2])
        ve = sb("ve", [128, B])
        rstd = sb("rstd", [128, B])
        shift_t = sb("shift_t", [128, B])
        scale1 = sb("scale1", [128, B])
        shift1 = sb("shift1", [128, B])
        scale2 = sb("scale2", [128, B])
        shift2 = sb("shift2", [128, B])

        xn = win[:, 0:RING * N].rearrange("p (r n) -> p r n", r=RING)
        xn_hi = sb("xn_hi", [128, RING, N], F32R)
        xn_lo = sb("xn_lo", [128, RING, N], F32R)
        qk_parts = sb("qk_parts", [128, 2, 2, 2, N], F32R)
        q_stack = [sb(f"q_stack{r}", [128, HEADS, N], F32R) for r in range(RING)]
        k_stack = [sb(f"k_stack{r}", [128, HEADS, N], F32R) for r in range(RING)]
        v_aug = sb("v_aug", [128, RING, 2, HEADS, 32])
        neg_max = sb("neg_max", [128, 2, 2, HALF])
        max_row = sb("max_row", [HALF, 2, N], F32R)
        probs = up_t[:, 0:2 * HALF * 2 * N].rearrange("p (u h c n) -> p u h c n", u=2, h=HALF, c=2)
        attn = up_t[:, 4096:4096 + B * N].rearrange("p (b n) -> p b n", b=B)
        sums = sb("sums", [128, 2, N])
        inv = sb("inv", [128, 2 * HEADS])
        inv_wide = sb("inv_wide", [128, 2, 2, 128])
        weighted = sb("weighted", [128, 2, N])

        xm = up_t[:, 6144:6144 + B * N]
        xm_hi = sb("xm_hi", [128, B * N], F32R)
        xm_lo = sb("xm_lo", [128, B * N], F32R)
        tanh_h = win[:, 1024:2048].rearrange("p (r n) -> p r n", r=MLP_RING)
        swish = win[:, 2048:3072].rearrange("p (r n) -> p r n", r=MLP_RING)
        gated = win[:, 5120:6144].rearrange("p (r n) -> p r n", r=MLP_RING)
        gated_hi = sb("gated_hi", [128, MLP_RING, N], F32R)
        gated_lo = sb("gated_lo", [128, MLP_RING, N], F32R)
        result = win[:, 3072:3072 + B * N]

        def pb(name, banks):
            return ctx.enter_context(nc.psum_tensor(name, [128, banks, 512], F32))
        pm = pb("pm", 2)
        ps = pb("ps", 2)
        po = pb("po", 1)
        px = pb("px", 1)
        pf = pb("pf", 2)
        up_bank = [ps[:, 0, :], ps[:, 1, :], pf[:, 0, :], pf[:, 1, :]]

        def down_bank(b):
            return pm[:, b % 2, 0:N] if b < B // 2 else (po[:, 0, 0:N], pf[:, 1, 0:N])[b % 2]

        def gn_bank(n):
            return po[:, 0, :] if n < 2 else pf[:, 0, :] if n < 6 else ps[:, 1, :]

        FIRST_TURN = HC * MLP_LAG

        def hidden_bank(n):
            return pf[:, 0, :] if n < FIRST_TURN else (pf[:, 0, :], pm[:, 0, :], pm[:, 1, :])[(n - FIRST_TURN) % 3]

        def hidden_before(n):
            return n - 1 if n <= FIRST_TURN else n - 3 if n >= FIRST_TURN + 3 else None

        def acc_bank(i):
            return pf[:, 1, 0:N] if i <= MLP_LAG or i % 2 == 0 else ps[:, 0, 0:N]

        fac_in = sem("fac_in")
        bias_in = sem("bias_in")
        vec_in = sem("vec_in")
        const_in = sem("const_in")
        wqk_in = sem("wqk_in")
        w_in = sem("w_in")
        wmlp_in = sem("wmlp_in")
        win_in = [[sem(f"win_in{t}{h}") for h in range(2)] for t in range(NWIN)]
        kron_ready = sem("kron_ready")
        biased_dve, biased_pool = sem("biased_dve"), sem("biased_pool")
        up_done = sem("up_done")
        neg_ready = sem("neg_ready")
        up_ready = sem("up_ready")
        down_done = sem("down_done")
        y_ready = sem("y_ready")
        bn_raw = sem("bn_raw")
        mean_ready = sem("mean_ready")
        gn_step = sem("gn_step")
        gn_done = sem("gn_done")
        gn_read = sem("gn_read")
        gn_var = sem("gn_var")
        gn_rstd = sem("gn_rstd")
        gn_ready = sem("gn_ready")
        pool_step = sem("pool_step")
        wqk_split = sem("wqk_split")
        wmlp_split = sem("wmlp_split")
        rest_ready = sem("rest_ready")
        consts_ready = sem("consts_ready")
        stacks_clear = sem("stacks_clear")
        xn_made = sem("xn_made")
        xn_ready = sem("xn_ready")
        qk_done = sem("qk_done")
        qk_hi = sem("qk_hi")
        qk_lo = sem("qk_lo")
        stack_in = [sem(f"stack_in{r}") for r in range(RING)]
        v_done = sem("v_done")
        v_ready = sem("v_ready")
        max_done = sem("max_done")
        max_read = sem("max_read")
        turn_done = sem("turn_done")
        rows_read = sem("rows_read")
        row_in = [sem("row_in0"), sem("row_in1")]
        scores_done = sem("scores_done")
        probs_ready = sem("probs_ready")
        pv_done = sem("pv_done")
        sums_ready = sem("sums_ready")
        den_done = sem("den_done")
        inv_ready = sem("inv_ready")
        inv_wide_ready = sem("inv_wide_ready")
        inv_done = sem("inv_done")
        weighted_ready = sem("weighted_ready")
        proj_done = sem("proj_done")
        attn_ready = sem("attn_ready")
        xm_made = sem("xm_made")
        xm_ready = sem("xm_ready")
        hidden_done = sem("hidden_done")
        tanh_ready = sem("tanh_ready")
        swish_ready = sem("swish_ready")
        gated_made = sem("gated_made")
        hi_made = sem("hi_made")
        gated_ready = sem("gated_ready")
        mlp_done = sem("mlp_done")
        result_ready = sem("result_ready")
        stored = sem("stored")

        block = ctx.enter_context(nc.Block())

        @block.sync
        def _(sp):
            sp.dma_start(bias_bc[:, :], bass.AP(tensor=bias0.tensor, offset=0, ap=[[0, 128], [1, C]])).then_inc(bias_in, 16)
            for half in range(2):
                for t in range(NWIN):
                    r0 = WINDOW_ROWS[t] * W
                    sp.dma_start(win_at(t, half), xw[r0:r0 + 128, half * BH:(half + 1) * BH]).then_inc(win_in[t][half], 16)
            sp.dma_start(vec[:, :], vecs).then_inc(vec_in, 16)
            sp.dma_start(ident_s[:, :], ident).then_inc(const_in, 16)
            sp.dma_start(gmat_s[:, :], gmat).then_inc(const_in, 16)
            sp.dma_start(wqk_s[:, :], wqk).then_inc(wqk_in, 16)
            sp.dma_start(wv_s[:, :], wv).then_inc(w_in, 16)
            sp.dma_start(wo_s[:, :, :], wo).then_inc(w_in, 16)
            sp.dma_start(bv_bc[:, :], bass.AP(tensor=bv.tensor, offset=0, ap=[[0, 128], [1, C]])).then_inc(w_in, 16)
            sp.dma_start(w1_s[:, :], w1).then_inc(wmlp_in, 16)
            sp.dma_start(w2_s[:, :], w2).then_inc(wmlp_in, 16)

            def stack(i, k):
                if i < RING:
                    sp.wait_ge(stacks_clear, 2 * (i + 1))
                else:
                    sp.wait_ge(scores_done, HEADS * (i - 2))
                for part, ready, rows in ((0, qk_hi, ((0, 1), (0, 2))), (1, qk_lo, ((2,), (1,)))):
                    for j, s in enumerate((q_stack, k_stack)):
                        sp.wait_ge(ready, 2 * i + j + 1)
                        for r in rows[j]:
                            sp.dma_start(s[k][r * D:(r + 1) * D, :, :].bitcast(F32),
                                         qk_parts[:, i % 2, j, part, :].bitcast(F32)).then_inc(stack_in[k], 16)

            for i in range(B):
                stack(i, i % RING)
            for b in range(B):
                sp.wait_ge(result_ready, b + 1)
                sp.dma_start(out[b], result[:, b * N:(b + 1) * N]).then_inc(stored, 16)
            sp.wait_ge(stored, 16 * B)

        @block.gpsimd
        def _(pool):
            steps = 0

            def split(hi, lo, src):
                nonlocal steps
                pool.tensor_scalar(hi, src, 1.0, 0.0, ALU.mult, ALU.add).then_inc(pool_step, 1)
                steps += 1
                pool.wait_ge(pool_step, steps)
                return pool.tensor_tensor(lo, src, hi.bitcast(F32), ALU.subtract)

            pool.dma_start(fac[:, :], factors).then_inc(fac_in, 16)
            pool.wait_ge(bias_in, 16)

            def add_bias(n):
                t, half = POOL_WINDOWS[n]
                pool.wait_ge(win_in[t][half], 16)
                x4 = win_at(t, half).rearrange("p (b c) -> p b c", c=C)
                pool.tensor_tensor(x4, x4, bias_bc[:, None, :].to_broadcast([128, B // 2, C]), ALU.add).then_inc(biased_pool, 1)

            def rsqrt(n):
                b0, b1 = GN_BATCHES[n]
                pool.wait_ge(gn_var, n + 1)
                pool.tensor_tensor(rstd[:, b0:b1], ve[:, b0:b1], half_neg[:, b0:b1], ALU.pow).then_inc(gn_rstd, 1)

            def normalise(i):
                k = i % RING
                pool.wait_ge(gn_ready, 1 if i == 0 else 2 if i < B // 2 else 3)
                if i >= RING:
                    pool.wait_ge(qk_done, i - RING + 1)
                    pool.wait_ge(v_done, i - RING + 1)
                pool.tensor_scalar(xn[:, k, :], y[:, i, :], scale_of(scale1, i), scale_of(shift1, i),
                                   ALU.mult, ALU.add).then_inc(xn_made, 1)
                pool.wait_ge(xn_made, 2 * i + 1)
                pool.tensor_scalar(xn_hi[:, k, :], xn[:, k, :], 1.0, 0.0, ALU.mult, ALU.add).then_inc(xn_made, 1)
                pool.wait_ge(xn_made, 2 * i + 2)
                pool.tensor_tensor(xn_lo[:, k, :], xn[:, k, :], xn_hi[:, k, :].bitcast(F32), ALU.subtract).then_inc(xn_ready, 1)

            def scale_of(tile, i):
                return tile[:, bass.ds(i, 1)] if not isinstance(i, int) else tile[:, i:i + 1]

            def rows(i, half):
                pool.wait_ge(rows_read, 2 * i + half + 1)
                pool.dma_start(q_stack[i % RING][ROW:ROW + 1, half * HALF:(half + 1) * HALF, :].bitcast(F32),
                               max_row[:, half, :].bitcast(F32)).then_inc(row_in[half], 16)

            def split_wqk():
                pool.wait_ge(wqk_in, 16)
                split(wqk_hi[:, :], wqk_lo[:, :], wqk_s[:, :]).then_inc(wqk_split, 1)

            def split_w1():
                pool.wait_ge(wmlp_in, 32)
                split(w1_hi[:, :], w1_lo[:, :], w1_s[:, :]).then_inc(wmlp_split, 1)

            def split_w2():
                split(w2_hi[:, :], w2_lo[:, :], w2_s[:, :]).then_inc(wmlp_split, 1)

            def constants():
                pool.memset(half_neg[:, :], -0.5).then_inc(consts_ready, 1)
                pool.memset(v_aug[:, :, :, :, :], 0.0).then_inc(consts_ready, 1)
                pool.wait_ge(consts_ready, 2)
                pool.memset(v_aug[:, :, :, :, D:D + 1], 1.0).then_inc(consts_ready, 1)

            def second_norm(i):
                cols = slice(i * N, (i + 1) * N)
                pool.wait_ge(gn_ready, [n for n, (_, end) in enumerate(GN_BATCHES) if n >= len(GN1_BATCHES) and i < end][0] + 1)
                pool.tensor_scalar(xm[:, cols], attn[:, i, :], scale2[:, i:i + 1], shift2[:, i:i + 1],
                                   ALU.mult, ALU.add).then_inc(xm_made, 1)
                pool.tensor_scalar(xm_hi[:, cols], attn[:, i, :], scale2[:, i:i + 1], shift2[:, i:i + 1],
                                   ALU.mult, ALU.add).then_inc(xm_made, 1)
                pool.wait_ge(xm_made, 2 * i + 2)
                pool.tensor_tensor(xm_lo[:, cols], xm[:, cols], xm_hi[:, cols].bitcast(F32), ALU.subtract).then_inc(xm_ready, 1)

            def gated_low(n):
                pool.wait_ge(hi_made, n + 1)
                pool.tensor_tensor(gated_lo[:, n % MLP_RING, :], gated[:, n % MLP_RING, :],
                                   gated_hi[:, n % MLP_RING, :].bitcast(F32), ALU.subtract).then_inc(gated_ready, 1)

            add_bias(0)
            constants()
            add_bias(1)
            add_bias(2)
            add_bias(3)
            add_bias(4)
            add_bias(5)
            split_wqk()
            rsqrt(0)
            normalise(0)
            add_bias(6)
            add_bias(7)
            rsqrt(1)
            normalise(1)
            normalise(2)
            split_w1()
            rows(0, 0)
            rows(0, 1)
            for i in range(B):
                nxt, n = i + 1 < B, HC * (i - MLP_LAG)
                if i + RING < B:
                    normalise(i + RING)
                if nxt:
                    rows(i + 1, 0)
                if n >= 0:
                    gated_low(n)
                if i in (3, 5, 7):
                    rsqrt(3 + (i - 3) // 2)
                if n >= 0:
                    gated_low(n + 1)
                    gated_low(n + 2)
                if i == 0:
                    rsqrt(2)
                if i in (3, 5, 7):
                    second_norm(i - 3)
                if i == 1:
                    split_w2()
                if nxt:
                    rows(i + 1, 1)
                if n >= 0:
                    gated_low(n + 3)
                if i in (3, 5, 7):
                    second_norm(i - 2)
            rsqrt(6)
            gated_low(16)
            second_norm(6)
            gated_low(17)
            gated_low(18)
            gated_low(19)
            gated_low(20)
            gated_low(21)
            rsqrt(7)
            gated_low(22)
            second_norm(7)
            gated_low(23)
            gated_low(24)
            gated_low(25)
            gated_low(26)
            gated_low(27)
            gated_low(28)
            gated_low(29)
            gated_low(30)
            gated_low(31)

        @block.scalar
        def _(act):
            def fill(stack, column):
                act.activation(stack[:, :, :].rearrange("p h n -> p (h n)"),
                               rest[:, column:column + 1].to_broadcast([128, HEADS * N]), ACT.Copy).then_inc(stacks_clear, 1)

            def negative(n):
                act.wait_ge(up_done, n + 1)
                if n >= 2:
                    act.wait_ge(up_ready, n - 1)
                act.activation(lrelu_neg[:, n % 2, :], up_bank[n % 4], ACT.Copy,
                               scale=SLOPE * GAIN * UPGAIN).then_inc(neg_ready, 1)

            def read_y(b):
                act.wait_ge(down_done, b + 1)
                act.activation(y[:, b, :], down_bank(b), ACT.Copy).then_inc(y_ready, 1)

            def high_parts(i):
                act.wait_ge(vec_in, 16)
                act.wait_ge(qk_done, i + 1)
                if i >= 2:
                    act.wait_ge(stack_in[(i - 2) % RING], 32 * STACKED * ((i - 2) // RING + 1))
                act.activation(qk_parts[:, i % 2, 0, 0, :], px[:, 0, 0:N], ACT.Identity, bias=bq).then_inc(qk_hi, 1)
                act.activation(qk_parts[:, i % 2, 1, 0, :], px[:, 0, N:2 * N], ACT.Identity, bias=bk).then_inc(qk_hi, 1)

            def exponentials(i, h):
                act.wait_ge(scores_done, HEADS * i + h + 1)
                if i:
                    act.wait_ge(pv_done, 2 * (i - 1) + h // HALF + 1)
                act.activation(probs[:, h // HALF, h % HALF, :, :].rearrange("p c n -> p (c n)"),
                               ps[:, h % 2, :], ACT.Exp, scale=D ** -0.5).then_inc(probs_ready, 1)

            def read_sums(i):
                act.wait_ge(pv_done, 2 * (i + 1))
                if i:
                    act.wait_ge(weighted_ready, i)
                act.activation(sums[:, :, :].rearrange("p a n -> p (a n)"), po[:, 0, :], ACT.Copy).then_inc(sums_ready, 1)

            def spread_inverse(i):
                act.wait_ge(inv_ready, i + 1)
                if i:
                    act.wait_ge(inv_done, i)
                act.activation(inv_wide[:, :, :, :].rearrange("p c a (g d) -> p (c a g) d", d=32),
                               inv[:, :, None].to_broadcast([128, 2 * HEADS, 32]), ACT.Copy).then_inc(inv_wide_ready, 1)

            def read_proj(i):
                act.wait_ge(proj_done, i + 1)
                dst = attn[:, i, :] if isinstance(i, int) else attn[:, bass.ds(i, 1), :].rearrange("p a n -> p (a n)")
                act.activation(dst, px[:, 0, 0:N], ACT.Identity, bias=bo).then_inc(attn_ready, 1)

            def read_rows(i, half):
                act.wait_ge(turn_done, 2 * i + half + 1)
                if i:
                    act.wait_ge(row_in[half], 16 * i)
                act.activation(max_row[:, half, :], pm[0:HALF, 1, 0:N], ACT.Copy).then_inc(rows_read, 1)

            def tanh_half(n):
                act.wait_ge(hidden_done, n + 1)
                if n >= MLP_RING:
                    act.wait_ge(swish_ready, n - MLP_RING + 1)
                act.activation(tanh_h[:, n % MLP_RING, :], hidden_bank(n)[:, 0:N], ACT.Tanh, scale=0.5).then_inc(tanh_ready, 1)

            def gated_high(n):
                act.wait_ge(gated_made, n + 1)
                if n >= MLP_RING:
                    act.wait_ge(mlp_done, n - MLP_RING + 1)
                act.activation(gated_hi[:, n % MLP_RING, :], gated[:, n % MLP_RING, :], ACT.Copy).then_inc(hi_made, 1)

            act.wait_ge(rest_ready, 2)
            fills = [(s[r], c) for r in range(RING) for s, c in ((q_stack, 1), (k_stack, 0))]
            fill(*fills[0])
            fill(*fills[1])
            negative(0)
            negative(1)
            negative(2)
            negative(3)
            negative(4)
            negative(5)
            negative(6)
            negative(7)
            negative(8)
            read_y(0)
            fill(*fills[2])
            read_y(1)
            negative(9)
            negative(10)
            read_y(2)
            read_y(3)
            high_parts(0)
            negative(11)
            negative(12)
            negative(13)
            negative(14)
            negative(15)
            high_parts(1)
            read_y(4)
            fill(*fills[3])
            read_y(5)
            fill(*fills[4])
            read_rows(0, 0)
            read_y(6)
            fill(*fills[5])
            read_y(7)
            read_rows(0, 1)
            for i in range(B):
                nxt, prev, n = i + 1 < B, i >= 1, HC * (i - MLP_LAG)
                if i >= 2:
                    read_proj(i - 2)
                exponentials(i, 0)
                if i + 2 < B:
                    high_parts(i + 2)
                if n >= 0:
                    tanh_half(n)
                exponentials(i, 1)
                exponentials(i, 2)
                if prev:
                    read_sums(i - 1)
                exponentials(i, 3)
                if n >= 0:
                    tanh_half(n + 1)
                exponentials(i, 4)
                if nxt:
                    read_rows(i + 1, 0)
                if n >= 0:
                    gated_high(n)
                exponentials(i, 5)
                if n >= 0:
                    gated_high(n + 1)
                if prev:
                    spread_inverse(i - 1)
                if n >= 0:
                    tanh_half(n + 2)
                exponentials(i, 6)
                if n >= 0:
                    gated_high(n + 2)
                exponentials(i, 7)
                if n >= 0:
                    tanh_half(n + 3)
                if nxt:
                    read_rows(i + 1, 1)
                if n >= 0:
                    gated_high(n + 3)
            read_proj(B - 2)
            tanh_half(16)
            read_sums(B - 1)
            tanh_half(17)
            gated_high(16)
            tanh_half(18)
            spread_inverse(B - 1)
            gated_high(17)
            tanh_half(19)
            tanh_half(20)
            gated_high(18)
            tanh_half(21)
            gated_high(19)
            read_proj(B - 1)
            tanh_half(22)
            gated_high(20)
            gated_high(21)
            tanh_half(23)
            gated_high(22)
            tanh_half(24)
            gated_high(23)
            tanh_half(25)
            tanh_half(26)
            gated_high(24)
            tanh_half(27)
            gated_high(25)
            tanh_half(28)
            gated_high(26)
            tanh_half(29)
            gated_high(27)
            gated_high(28)
            tanh_half(30)
            gated_high(29)
            tanh_half(31)
            gated_high(30)
            gated_high(31)

        @block.tensor
        def _(pe):
            def three(dst, w_hi, w_lo, x_hi, x_lo, start, stop):
                pe.matmul(dst, w_hi, x_hi, start=start, stop=False)
                pe.matmul(dst, w_hi, x_lo, start=False, stop=False)
                return pe.matmul(dst, w_lo, x_hi, start=False, stop=stop)

            def upsample(n):
                half, m = divmod(n, CHUNKS)
                window = (WINDOW_OF[m], half)
                if window in DVE_WINDOWS:
                    pe.wait_ge(biased_dve, DVE_WINDOWS.index(window) + 1)
                else:
                    pe.wait_ge(biased_pool, POOL_WINDOWS.index(window) + 1)
                pe.wait_ge(kron_ready, UP_WEIGHT_OF[m] + 1)
                if n >= 4:
                    pe.wait_ge(up_ready, n - 3)
                pe.matmul(up_bank[n % 4], up_w[:, UP_WEIGHT_OF[m], :, :].rearrange("p a b -> p (a b)"),
                          win_at(WINDOW_OF[m], half), start=True, stop=True).then_inc(up_done, 1)

            def group_means(n):
                b0, b1 = GN_BATCHES[n]
                if n < 2:
                    pe.wait_ge(const_in, 32)
                if n == 1:
                    pe.wait_ge(gn_read, 1)
                if n in (4, 5):
                    pe.wait_ge(gated_made, 2 * HC * (n - 4) + HC + 2)
                if n >= 6:
                    pe.wait_ge(probs_ready, HEADS * B)
                pe.wait_ge(mean_ready, n + 1)
                pe.matmul(gn_bank(n)[:, 0:2 * (b1 - b0)], gmat_s[:, :], mv[:, b0:b1, :].rearrange("p b s -> p (b s)"),
                          start=True, stop=True).then_inc(gn_done, 1)

            def downsample(b):
                half = b // (B // 2)
                if b == 0:
                    pe.wait_ge(kron_ready, UP_VARIANTS + 1)
                if b == 4:
                    pe.wait_ge(gn_read, 2)
                if b in (2, 3, 6, 7):
                    pe.wait_ge(y_ready, b - 1)
                col = (b % (B // 2)) * C
                for m in range(CHUNKS):
                    pe.wait_ge(up_ready, CHUNKS * half + m + 1)
                    o0, o1 = max(0, 2 * m - 3), min(W, 2 * m + 5)
                    mm = pe.matmul(down_bank(b)[:, o0 * W:o1 * W], up_at(m, half)[:, col:col + C],
                                   dn_w[:, o0 - 2 * m + 3:o1 - 2 * m + 3, :].rearrange("p a b -> p (a b)"),
                                   start=(m == 0), stop=(m == CHUNKS - 1), skip_group_check=True)
                mm.then_inc(down_done, 1)

            def project_qk(i):
                pe.wait_ge(wqk_split, 1)
                pe.wait_ge(xn_ready, i + 1)
                if i:
                    pe.wait_ge(v_ready, i)
                if i >= 4:
                    pe.wait_ge(attn_ready, i - 3)
                for j in range(2):
                    mm = three(px[:, 0, j * N:(j + 1) * N], wqk_hi[:, j * C:(j + 1) * C], wqk_lo[:, j * C:(j + 1) * C],
                               xn_hi[:, i % RING, :], xn_lo[:, i % RING, :], True, True)
                mm.then_inc(qk_done, 1)

            def project_v(i):
                pe.wait_ge(w_in, 48)
                pe.wait_ge(qk_lo, 2 * (i + 1))
                for c in range(2):
                    mm = pe.matmul(px[:, 0, c * C:(c + 1) * C], xn[:, i % RING, c * 128:(c + 1) * 128], wv_s[:, :],
                                   start=True, stop=True)
                mm.then_inc(v_done, 1)

            def maxima(i, h):
                k = i % RING
                if h == 0:
                    pe.wait_ge(stack_in[k], 32 * STACKED * (i // RING + 1))
                    if i == 0:
                        pe.wait_ge(y_ready, B // 2)
                if h == 0 and i:
                    pe.wait_ge(max_read, HEADS * i)
                if h == 1 and i:
                    pe.wait_ge(rows_read, 2 * i)
                if h in (2, 3, 4):
                    pe.wait_ge(max_read, HEADS * i + h - 1)
                if h == 5:
                    pe.wait_ge(max_read, HEADS * i + 5)
                if h == 6:
                    pe.wait_ge(rows_read, 2 * i + 1)
                if h == 7:
                    pe.wait_ge(max_read, HEADS * i + 6)
                for c in range(2):
                    mm = pe.matmul(pm[:, MAX_BANK[h], c * N:(c + 1) * N], q_stack[k][:, h, c * 128:(c + 1) * 128],
                                   k_stack[k][:, h, :], start=True, stop=True)
                mm.then_inc(max_done, 1)

            def turn_maxima(i, half):
                pe.wait_ge(max_read, HEADS * i + HALF * (half + 1))
                for c in range(2):
                    mm = pe.transpose(pm[0:HALF, 1, c * 128:(c + 1) * 128], neg_max[:, half, c, :], ident_s[:, :])
                mm.then_inc(turn_done, 1)

            def scores(i, h):
                if h % HALF == 0:
                    pe.wait_ge(row_in[h // HALF], 16 * (i + 1))
                if HEADS * i + h >= 2:
                    pe.wait_ge(probs_ready, HEADS * i + h - 1)
                for c in range(2):
                    mm = pe.matmul(ps[:, h % 2, c * N:(c + 1) * N], k_stack[i % RING][:, h, c * 128:(c + 1) * 128],
                                   q_stack[i % RING][:, h, :], start=True, stop=True)
                mm.then_inc(scores_done, 1)

            def weigh(i, half, c):
                if c == 0:
                    pe.wait_ge(probs_ready, HEADS * i + HALF * (half + 1))
                    pe.wait_ge(v_ready, i + 1)
                    if half == 0 and i:
                        pe.wait_ge(sums_ready, i)
                    elif half == 0:
                        pe.wait_ge(y_ready, B)
                for g in range(HALF):
                    mm = pe.matmul(po[32 * g:32 * g + 32, 0, half * N:(half + 1) * N],
                                   v_aug[:, i % RING, c, half * HALF + g, :], probs[:, half, g, c, :],
                                   start=(c == 0), stop=(c == 1), skip_group_check=True)
                if c == 1:
                    mm.then_inc(pv_done, 1)

            def turn_sums(i):
                pe.wait_ge(sums_ready, i + 1)
                if i + 3 < B:
                    pe.wait_ge(v_ready, i + 4)
                elif i:
                    pe.wait_ge(attn_ready, i)
                for c in range(2):
                    for half in range(2):
                        a = (2 * c + half) * 128
                        mm = pe.transpose(px[:, 0, a:a + 128], sums[:, half, c * 128:(c + 1) * 128], ident_s[:, :])
                mm.then_inc(den_done, 1)

            def turn_inverse(i):
                pe.wait_ge(inv_wide_ready, i + 1)
                for half in range(2):
                    for c in range(2):
                        mm = pe.transpose(px[:, 0, half * N + c * 128:half * N + (c + 1) * 128],
                                          inv_wide[:, c, half, :], ident_s[:, :])
                mm.then_inc(inv_done, 1)

            def project_out(i):
                pe.wait_ge(weighted_ready, i + 1)
                for half in range(2):
                    mm = pe.matmul(px[:, 0, 0:N], wo_s[:, half, :], weighted[:, half, :], start=(half == 0), stop=(half == 1))
                mm.then_inc(proj_done, 1)

            def hidden(n):
                i, hc = divmod(n, HC)
                if hc == 0:
                    pe.wait_ge(wmlp_split, 1)
                    pe.wait_ge(xm_ready, i + 1)
                if n in (HC + 2, 3 * HC + 2):
                    pe.wait_ge(gn_read, 5 + n // (2 * HC))
                before = hidden_before(n)
                if before is None:
                    pe.wait_ge(rows_read, 2 * B)
                elif before >= 0:
                    pe.wait_ge(gated_made, before + 1)
                cols = slice(i * N, (i + 1) * N)
                for j in range(2):
                    a = j * HIDDEN + hc * C
                    mm = three(hidden_bank(n)[:, j * N:(j + 1) * N], w1_hi[:, a:a + C], w1_lo[:, a:a + C],
                               xm_hi[:, cols], xm_lo[:, cols], True, True)
                mm.then_inc(hidden_done, 1)

            def down_project(n):
                i, hc = divmod(n, HC)
                pe.wait_ge(gated_ready, n + 1)
                if hc == 0:
                    pe.wait_ge(wmlp_split, 2)
                    if i == MLP_LAG + 1:
                        pe.wait_ge(probs_ready, HEADS * B)
                    elif i:
                        pe.wait_ge(result_ready, i if i <= MLP_LAG else i - 1)
                three(acc_bank(i), w2_hi[:, hc * C:(hc + 1) * C], w2_lo[:, hc * C:(hc + 1) * C],
                      gated_hi[:, n % MLP_RING, :], gated_lo[:, n % MLP_RING, :], hc == 0, hc == HC - 1).then_inc(mlp_done, 1)

            upsample(0)
            upsample(1)
            upsample(2)
            upsample(3)
            upsample(4)
            upsample(5)
            upsample(6)
            upsample(7)
            upsample(8)
            downsample(0)
            upsample(9)
            downsample(1)
            group_means(0)
            upsample(10)
            downsample(2)
            downsample(3)
            project_qk(0)
            group_means(1)
            upsample(11)
            upsample(12)
            upsample(13)
            project_v(0)
            upsample(14)
            upsample(15)
            project_qk(1)
            downsample(4)
            maxima(0, 0)
            maxima(0, 1)
            downsample(5)
            maxima(0, 2)
            maxima(0, 3)
            downsample(6)
            maxima(0, 4)
            turn_maxima(0, 0)
            project_v(1)
            maxima(0, 5)
            maxima(0, 6)
            downsample(7)
            maxima(0, 7)
            turn_maxima(0, 1)

            for i in range(B):
                nxt, prev, qkv, n = i + 1 < B, i >= 1, i + 2 < B, HC * (i - MLP_LAG)
                if nxt:
                    maxima(i + 1, 0)
                scores(i, 0)
                scores(i, 1)
                if nxt:
                    maxima(i + 1, 1)
                if qkv:
                    project_qk(i + 2)
                if i == 0:
                    group_means(2)
                if nxt:
                    maxima(i + 1, 2)
                if n >= 0:
                    hidden(n)
                scores(i, 2)
                if prev:
                    weigh(i - 1, 1, 0)
                    weigh(i - 1, 1, 1)
                if nxt:
                    maxima(i + 1, 3)
                scores(i, 3)
                if nxt:
                    maxima(i + 1, 4)
                if qkv:
                    project_v(i + 2)
                if n >= 0:
                    hidden(n + 1)
                scores(i, 4)
                if nxt:
                    turn_maxima(i + 1, 0)
                scores(i, 5)
                if nxt:
                    maxima(i + 1, 5)
                if prev:
                    turn_sums(i - 1)
                weigh(i, 0, 0)
                if i in (3, 5, 7):
                    group_means(3 + (i - 3) // 2)
                if nxt:
                    maxima(i + 1, 6)
                scores(i, 6)
                if n >= 1:
                    down_project(n - 1)
                if n >= 0:
                    hidden(n + 2)
                if nxt:
                    maxima(i + 1, 7)
                scores(i, 7)
                if n >= 0:
                    down_project(n)
                if prev:
                    turn_inverse(i - 1)
                weigh(i, 0, 1)
                if n >= 0:
                    hidden(n + 3)
                if prev:
                    project_out(i - 1)
                if nxt:
                    turn_maxima(i + 1, 1)
                if n >= 0:
                    down_project(n + 1)
                    down_project(n + 2)

            weigh(B - 1, 1, 0)
            weigh(B - 1, 1, 1)
            hidden(16)
            group_means(6)
            hidden(17)
            turn_sums(B - 1)
            hidden(18)
            hidden(19)
            turn_inverse(B - 1)
            down_project(15)
            hidden(20)
            hidden(21)
            down_project(16)
            project_out(B - 1)
            down_project(17)
            hidden(22)
            down_project(18)
            hidden(23)
            group_means(7)
            hidden(24)
            hidden(25)
            down_project(19)
            down_project(20)
            hidden(26)
            down_project(21)
            hidden(27)
            down_project(22)
            hidden(28)
            hidden(29)
            down_project(23)
            down_project(24)
            hidden(30)
            down_project(25)
            hidden(31)
            down_project(26)
            down_project(27)
            down_project(28)
            down_project(29)
            down_project(30)
            down_project(31)

        @block.vector
        def _(dve):
            steps = 0

            def chain(ins):
                nonlocal steps
                steps += 1
                ins.then_inc(gn_step, 1)
                dve.wait_ge(gn_step, steps)

            dve.memset(rest[:, :], 0.0).then_inc(rest_ready, 1)
            dve.wait_ge(rest_ready, 1)
            dve.memset(rest[ROW:ROW + 1, 0:1], 1.0).then_inc(rest_ready, 1)
            fast = fac[:, 0:32]
            slow = fac[:, 32:52].rearrange("p (v a) -> p v a", v=UP_VARIANTS)
            dve.wait_ge(fac_in, 16)
            dve.wait_ge(bias_in, 16)

            def up_weights(v):
                dve.tensor_tensor(up_w[:, v, :, :], slow[:, v, :, None].to_broadcast([128, 4, 32]),
                                  fast[:, None, :].to_broadcast([128, 4, 32]), ALU.mult).then_inc(kron_ready, 1)

            def down_weights():
                dve.tensor_tensor(dn_w[:, :, :], fac[:, 68:76, None].to_broadcast([128, 8, 16]),
                                  fac[:, None, 52:68].to_broadcast([128, 8, 16]), ALU.mult).then_inc(kron_ready, 1)

            def add_bias(n):
                t, half = DVE_WINDOWS[n]
                dve.wait_ge(win_in[t][half], 16)
                x4 = win_at(t, half).rearrange("p (b c) -> p b c", c=C)
                dve.tensor_tensor(x4, x4, bias_bc[:, None, :].to_broadcast([128, B // 2, C]), ALU.add).then_inc(biased_dve, 1)

            def leaky(n):
                dve.wait_ge(neg_ready, n + 1)
                dve.scalar_tensor_tensor(out=up_at(n % CHUNKS, n // CHUNKS), in0=up_bank[n % 4], scalar=GAIN * UPGAIN,
                                         in1=lrelu_neg[:, n % 2, :], op0=ALU.mult, op1=ALU.max).then_inc(up_ready, 1)

            def means(n):
                s = slice(*GN_BATCHES[n])
                if n >= len(GN1_BATCHES):
                    dve.wait_ge(bn_raw, 2 * GN_BATCHES[n][1])
                chain(dve.tensor_tensor(sq[:, s], mv[:, s, 0], mv[:, s, 0], ALU.mult))
                dve.tensor_tensor(mv[:, s, 1], mv[:, s, 1], sq[:, s], ALU.add).then_inc(mean_ready, 1)

            def variance(n):
                b0, b1 = GN_BATCHES[n]
                s = slice(b0, b1)
                dve.wait_ge(gn_done, n + 1)
                dve.tensor_copy(gs[:, s, :], gn_bank(n)[:, 0:2 * (b1 - b0)].rearrange("p (b s) -> p b s", s=2)).then_inc(gn_read, 1)
                dve.wait_ge(gn_read, n + 1)
                chain(dve.tensor_tensor(sq[:, s], gs[:, s, 0], gs[:, s, 0], ALU.mult))
                chain(dve.tensor_tensor(sq[:, s], gs[:, s, 1], sq[:, s], ALU.subtract))
                dve.tensor_scalar(ve[:, s], sq[:, s], EPS, None, ALU.add).then_inc(gn_var, 1)

            def coefficients(n):
                s = slice(*GN_BATCHES[n])
                if n < len(GN1_BATCHES):
                    gamma, beta, scale, shift = g1w, g1b, scale1, shift1
                else:
                    gamma, beta, scale, shift = g2w, g2b, scale2, shift2
                dve.wait_ge(vec_in, 16)
                dve.wait_ge(gn_rstd, n + 1)
                chain(dve.tensor_scalar(scale[:, s], rstd[:, s], gamma, None, ALU.mult))
                chain(dve.tensor_tensor(shift_t[:, s], gs[:, s, 0], scale[:, s], ALU.mult))
                dve.tensor_scalar(shift[:, s], shift_t[:, s], -1.0, beta, ALU.mult, ALU.add).then_inc(gn_ready, 1)

            def y_statistics(b):
                dve.wait_ge(y_ready, b + 1)
                chain(dve.bn_stats(stat6[:, b, :], y[:, b, :]))
                chain(dve.bn_aggr(mv[:, b, :], stat6[:, b, :]))

            def low_parts(i):
                dve.wait_ge(qk_hi, 2 * (i + 1))
                for j, bias in enumerate((bq, bk)):
                    dve.scalar_tensor_tensor(out=qk_parts[:, i % 2, j, 1, :], in0=px[:, 0, j * N:(j + 1) * N], scalar=bias,
                                             in1=qk_parts[:, i % 2, j, 0, :].bitcast(F32), op0=ALU.add,
                                             op1=ALU.subtract).then_inc(qk_lo, 1)

            def read_v(i):
                dve.wait_ge(v_done, i + 1)
                dve.wait_ge(w_in, 48)
                dve.wait_ge(consts_ready, 3)
                if i >= RING:
                    dve.wait_ge(pv_done, 2 * (i - 2))
                dve.tensor_tensor(v_aug[:, i % RING, :, :, 0:D], px[:, 0, 0:2 * C].rearrange("p (c h d) -> p c h d", c=2, d=D),
                                  bv_bc[:, :].rearrange("p (h d) -> p h d", d=D)[:, None, :, :].to_broadcast([128, 2, HEADS, D]),
                                  ALU.add).then_inc(v_ready, 1)

            def reduce_max(i, h):
                dve.wait_ge(max_done, HEADS * i + h + 1)
                if h % HALF == 0 and i:
                    dve.wait_ge(turn_done, 2 * i - 1 + h // HALF)
                dve.tensor_reduce(neg_max[:, h // HALF, :, h % HALF], pm[:, MAX_BANK[h], :].rearrange("p (c n) -> p c n", c=2),
                                  AX.X, ALU.max, negate=True).then_inc(max_read, 1)

            def invert(i):
                dve.wait_ge(den_done, i + 1)
                if i:
                    dve.wait_ge(inv_wide_ready, i)
                dve.reciprocal(inv[:, :], px[:, 0, :].rearrange("p (a d) -> p a d", d=32)[:, :, D]).then_inc(inv_ready, 1)

            def normalise(i):
                dve.wait_ge(inv_done, i + 1)
                if i:
                    dve.wait_ge(proj_done, i)
                dve.tensor_tensor(weighted[:, :, :].rearrange("p a n -> p (a n)"), px[:, 0, :],
                                  sums[:, :, :].rearrange("p a n -> p (a n)"), ALU.mult).then_inc(weighted_ready, 1)

            def statistics(i):
                ii = slice(i, i + 1) if isinstance(i, int) else bass.ds(i, 1)
                dve.wait_ge(attn_ready, i + 1)
                dve.bn_stats(stat6[:, ii, :].rearrange("p a s -> p (a s)"), attn[:, ii, :].rearrange("p a n -> p (a n)")).then_inc(bn_raw, 1)
                dve.wait_ge(bn_raw, 2 * i + 1)
                dve.bn_aggr(mv[:, ii, :].rearrange("p a s -> p (a s)"), stat6[:, ii, :].rearrange("p a s -> p (a s)")).then_inc(bn_raw, 1)

            def swish_gate(n):
                dve.wait_ge(tanh_ready, n + 1)
                dve.scalar_tensor_tensor(out=swish[:, n % MLP_RING, :], in0=tanh_h[:, n % MLP_RING, :], scalar=1.0,
                                         in1=hidden_bank(n)[:, 0:N], op0=ALU.add, op1=ALU.mult).then_inc(swish_ready, 1)
                dve.wait_ge(swish_ready, n + 1)
                if n >= MLP_RING:
                    dve.wait_ge(gated_ready, n - MLP_RING + 1)
                dve.scalar_tensor_tensor(out=gated[:, n % MLP_RING, :], in0=swish[:, n % MLP_RING, :], scalar=0.5,
                                         in1=hidden_bank(n)[:, N:2 * N], op0=ALU.mult, op1=ALU.mult).then_inc(gated_made, 1)

            def residual(i):
                dve.wait_ge(mlp_done, HC * (i + 1))
                dve.tensor_tensor(result[:, i * N:(i + 1) * N], acc_bank(i), y[:, i, :], ALU.add).then_inc(result_ready, 1)

            up_weights(0)
            add_bias(0)
            up_weights(1)
            add_bias(1)
            up_weights(2)
            up_weights(3)
            add_bias(2)
            leaky(0)
            add_bias(3)
            up_weights(4)
            leaky(1)
            leaky(2)
            down_weights()
            leaky(3)
            leaky(4)
            leaky(5)
            leaky(6)
            leaky(7)
            leaky(8)
            y_statistics(0)
            means(0)
            variance(0)
            leaky(9)
            coefficients(0)
            y_statistics(1)
            y_statistics(2)
            y_statistics(3)
            means(1)
            variance(1)
            low_parts(0)
            leaky(10)
            coefficients(1)
            leaky(11)
            read_v(0)
            leaky(12)
            leaky(13)
            leaky(14)
            leaky(15)
            low_parts(1)
            reduce_max(0, 0)
            reduce_max(0, 1)
            reduce_max(0, 2)
            reduce_max(0, 3)
            y_statistics(4)
            reduce_max(0, 4)
            y_statistics(5)
            reduce_max(0, 5)
            read_v(1)
            reduce_max(0, 6)
            reduce_max(0, 7)
            y_statistics(7)
            y_statistics(6)
            means(2)
            for i in range(B):
                nxt, prev, qkv, n = i + 1 < B, i >= 1, i + 2 < B, HC * (i - MLP_LAG)
                batch = 3 + (i - 3) // 2
                if nxt:
                    reduce_max(i + 1, 0)
                if i >= 2:
                    statistics(i - 2)
                if nxt:
                    reduce_max(i + 1, 1)
                    reduce_max(i + 1, 2)
                if qkv:
                    low_parts(i + 2)
                if n >= 0:
                    swish_gate(n)
                if nxt:
                    reduce_max(i + 1, 3)
                    reduce_max(i + 1, 4)
                if qkv:
                    read_v(i + 2)
                if i == 0:
                    variance(2)
                if i in (3, 5, 7):
                    means(batch)
                if n >= 0:
                    swish_gate(n + 1)
                if nxt:
                    reduce_max(i + 1, 5)
                if prev:
                    invert(i - 1)
                if i in (3, 5, 7):
                    variance(batch)
                if n >= 1:
                    residual(i - MLP_LAG - 1)
                if nxt:
                    reduce_max(i + 1, 6)
                if n >= 0:
                    swish_gate(n + 2)
                if prev:
                    normalise(i - 1)
                if nxt:
                    reduce_max(i + 1, 7)
                if i == 0:
                    coefficients(2)
                if i in (3, 5, 7):
                    coefficients(batch)
                if n >= 0:
                    swish_gate(n + 3)
            statistics(B - 2)
            means(6)
            variance(6)
            swish_gate(16)
            invert(B - 1)
            swish_gate(17)
            coefficients(6)
            swish_gate(18)
            normalise(B - 1)
            residual(B - MLP_LAG - 1)
            swish_gate(19)
            swish_gate(20)
            swish_gate(21)
            statistics(B - 1)
            means(7)
            swish_gate(22)
            variance(7)
            swish_gate(23)
            coefficients(7)
            swish_gate(24)
            swish_gate(25)
            swish_gate(26)
            residual(4)
            swish_gate(27)
            swish_gate(28)
            residual(5)
            swish_gate(29)
            swish_gate(30)
            swish_gate(31)
            residual(6)
            residual(B - 1)


def kernel(x, L0_conv_bias, L0_conv_up_filter, L0_conv_down_filter, L1_conv_gn1_gamma, L1_conv_gn1_beta,
           L1_conv_qkv_w, L1_conv_qkv_b, L1_conv_out_w, L1_conv_out_b, L1_conv_gn2_gamma, L1_conv_gn2_beta,
           L1_conv_mlp1_w, L1_conv_mlp2_w):
    import numpy as np
    import concourse.bacc as bacc
    from concourse.bass_utils import run_bass_kernel_spmd

    a = np.asarray

    def shifted(filt, rows, cols, tap):
        filt = a(filt)
        table = np.zeros((rows, cols), filt.dtype)
        for j in range(rows):
            for i in range(cols):
                if 0 <= tap(i, j) < filt.shape[0]:
                    table[j, i] = filt[tap(i, j)]
        return table

    up, down = L0_conv_up_filter, L0_conv_down_filter
    up_fast = np.tile(shifted(up, 16, 32, lambda i, j: 5 + i - 2 * j), (8, 1))
    slow = [shifted(up, 8, 4, lambda i, j, s=s: s + i - 2 * j) for s in (5, 9, 11, 13, 17)]
    up_slow = np.repeat(np.concatenate(slow, axis=1), 16, axis=0)
    dn_fast = np.tile(shifted(down, 32, 16, lambda o, r: 6 + 2 * o - r), (4, 1))
    dn_slow = np.repeat(shifted(down, 4, 8, lambda o, r: 2 * o - r), 32, axis=0)

    order = np.arange(C).reshape(HEADS, D).T.ravel()
    w, b = a(L1_conv_qkv_w), a(L1_conv_qkv_b)
    wqk = np.concatenate([w[0:C][order], w[C:2 * C][order]], axis=0).T
    wo = np.zeros((128, 2, C), w.dtype)
    for h in range(HEADS):
        wo[32 * (h % HALF):32 * (h % HALF) + D, h // HALF, :] = a(L1_conv_out_w)[:, h * D:(h + 1) * D].T
    vecs = np.zeros((128, 8), w.dtype)
    for j, v in enumerate((L1_conv_gn1_gamma, L1_conv_gn1_beta, L1_conv_gn2_gamma, L1_conv_gn2_beta,
                           b[0:C][order], b[C:2 * C][order], L1_conv_out_b)):
        vecs[:, j] = a(v)
    arrays = {
        "xw": a(x).transpose(2, 3, 0, 1).reshape(N, B * C),
        "factors": np.concatenate([up_fast, up_slow, dn_fast, dn_slow], axis=1),
        "bias0": a(L0_conv_bias), "vecs": vecs, "wqk": wqk, "wv": w[2 * C:].T, "bv": b[2 * C:],
        "wo": wo, "w1": a(L1_conv_mlp1_w).T,
        "w2": a(L1_conv_mlp2_w).T.reshape(HC, C, C).transpose(1, 0, 2).reshape(C, HC * C),
        "ident": np.eye(128, dtype=np.float32),
        "gmat": np.kron(np.eye(32, dtype=np.float32), np.full((4, 4), 0.25, np.float32)),
    }
    arrays = {f"in_{k}": np.ascontiguousarray(v) for k, v in arrays.items()}
    nc = bacc.Bacc("TRN2", target_bir_lowering=False, num_devices=1)
    ins = [nc.dram_tensor(k, v.shape, mybir.dt.from_np(v.dtype), kind="ExternalInput").ap() for k, v in arrays.items()]
    out = nc.dram_tensor("out", (B, C, N), F32, kind="ExternalOutput").ap()
    build(nc, *ins, out)
    r = run_bass_kernel_spmd(nc, [arrays], core_ids=[0])
    return r.results[0]["out"].reshape(B, C, W, W)
```

```python
from contextlib import ExitStack

import concourse.bass as bass
from concourse import mybir

F32 = mybir.dt.float32
F32R = mybir.dt.float32r
ALU = mybir.AluOpType
ACT = mybir.ActivationFunctionType
AX = mybir.AxisListType

B, C, W = 8, 128, 16
N = W * W
HEADS, D = 8, 16
HALF = HEADS // 2
HIDDEN = 4 * C
HC = HIDDEN // C
EPS = 1e-5
SLOPE = 0.2
GAIN = 1.4142135381698608
UPGAIN = 4.0
BH = B // 2 * C
CHUNKS = 8
WINDOW_ROWS = [0, 1, 3, 5, 7, 8]
WINDOW_OF = [0, 0, 1, 2, 3, 4, 5, 5]
UP_WEIGHT_OF = [0, 1, 2, 2, 2, 2, 3, 4]
UP_VARIANTS = 5
NWIN = len(WINDOW_ROWS)
DVE_WINDOWS = [(0, 0), (1, 0), (2, 0), (4, 0)]
POOL_WINDOWS = [(3, 0), (5, 0)] + [(t, 1) for t in range(NWIN)]
ROW = 64
RING = 3
STACKED = 3
WARM_UP = 4
MLP_RING = 4
MLP_LAG = 4
GN1_BATCHES = [(0, 1), (1, 4), (4, 8)]
GN2_BATCHES = [(0, 2), (2, 4), (4, 6), (6, 7), (7, 8)]
GN_BATCHES = GN1_BATCHES + GN2_BATCHES


def build(nc, xw, factors, bias0, vecs, wqk, wv, bv, wo, w1, w2,
          ident, gmat, out):
    ctx = ExitStack()
    with ctx:
        def sb(name, shape, dt=F32):
            return ctx.enter_context(nc.sbuf_tensor(name, shape, dt))

        def sem(name):
            return ctx.enter_context(nc.semaphore(name))

        ident_s = sb("ident_s", [128, 128])
        gmat_s = sb("gmat_s", [128, 128])
        fac = sb("fac", [128, 32 + 4 * UP_VARIANTS + 16 + 8])
        vec = sb("vec", [128, 8])
        g1w, g1b, g2w, g2b = (vec[:, j:j + 1] for j in range(4))
        bq, bk, bo = (vec[:, j:j + 1] for j in range(4, 7))
        bias_bc = sb("bias_bc", [128, C])
        bv_bc = sb("bv_bc", [128, C])
        up_w = sb("up_w", [128, UP_VARIANTS, 4, 32])
        dn_w = sb("dn_w", [128, 8, 16])
        wqk_s = sb("wqk_s", [128, 2 * C])
        wqk_hi = sb("wqk_hi", [128, 2 * C], F32R)
        wqk_lo = sb("wqk_lo", [128, 2 * C], F32R)
        wv_s = sb("wv_s", [128, C])
        wo_s = sb("wo_s", [128, 2, C])
        w1_s = sb("w1_s", [128, 2 * HIDDEN])
        w1_hi = sb("w1_hi", [128, 2 * HIDDEN], F32R)
        w1_lo = sb("w1_lo", [128, 2 * HIDDEN], F32R)
        w2_s = sb("w2_s", [128, HC * C])
        w2_hi = sb("w2_hi", [128, HC * C], F32R)
        w2_lo = sb("w2_lo", [128, HC * C], F32R)
        half_neg = sb("half_neg", [128, B])
        rest = sb("rest", [128, 2])

        win = sb("win", [128, NWIN * B * C])
        up_t = sb("up_t", [128, CHUNKS * B * C])
        lrelu_neg = sb("lrelu_neg", [128, 2, BH])
        y = sb("y", [128, B, N])

        def win_at(t, half):
            a = (t * 2 + half) * BH
            return win[:, a:a + BH]

        def up_at(m, half):
            a = (m * 2 + half) * BH
            return up_t[:, a:a + BH]

        stat6 = sb("stat6", [128, B, 6])
        mv = sb("mv", [128, B, 2])
        sq = sb("sq", [128, B])
        gs = sb("gs", [128, B, 2])
        ve = sb("ve", [128, B])
        rstd = sb("rstd", [128, B])
        shift_t = sb("shift_t", [128, B])
        scale1 = sb("scale1", [128, B])
        shift1 = sb("shift1", [128, B])
        scale2 = sb("scale2", [128, B])
        shift2 = sb("shift2", [128, B])

        xn = win[:, 0:RING * N].rearrange("p (r n) -> p r n", r=RING)
        xn_hi = sb("xn_hi", [128, RING, N], F32R)
        xn_lo = sb("xn_lo", [128, RING, N], F32R)
        qk_parts = sb("qk_parts", [128, 2, 2, 2, N], F32R)
        q_stack = [sb(f"q_stack{r}", [128, HEADS, N], F32R) for r in range(RING)]
        k_stack = [sb(f"k_stack{r}", [128, HEADS, N], F32R) for r in range(RING)]
        v_aug = sb("v_aug", [128, RING, 2, 2, D + HALF * 32])
        neg_max = sb("neg_max", [128, 2, HEADS])
        max_row = sb("max_row", [HEADS, N], F32R)
        probs = up_t[:, 0:2 * HALF * 2 * N].rearrange("p (u h c n) -> p u h c n", u=2, h=HALF, c=2)
        attn = up_t[:, 4096:4096 + B * N].rearrange("p (b n) -> p b n", b=B)
        sums = sb("sums", [128, 2, N])
        inv = sb("inv", [128, 2, HALF, 2])
        inv_wide = sb("inv_wide", [128, 2, 128])
        weighted = sb("weighted", [128, 2, N])

        xm = up_t[:, 6144:6144 + B * N]
        xm_hi = sb("xm_hi", [128, B * N], F32R)
        xm_lo = sb("xm_lo", [128, B * N], F32R)
        squashed = win[:, 1024:2048].rearrange("p (r n) -> p r n", r=MLP_RING)
        swish = win[:, 2048:3072].rearrange("p (r n) -> p r n", r=MLP_RING)
        gated = win[:, 5120:6144].rearrange("p (r n) -> p r n", r=MLP_RING)
        gated_hi = sb("gated_hi", [128, MLP_RING, N], F32R)
        gated_lo = sb("gated_lo", [128, MLP_RING, N], F32R)
        result = win[:, 3072:3072 + B * N]

        def pb(name, banks):
            return ctx.enter_context(nc.psum_tensor(name, [128, banks, 512], F32))
        pm = pb("pm", 2)
        ps = pb("ps", 2)
        po = pb("po", 1)
        px = pb("px", 1)
        pf = pb("pf", 2)
        up_bank = [ps[:, 0, :], ps[:, 1, :], pf[:, 0, :], pf[:, 1, :]]

        def down_bank(b):
            return pm[:, b % 2, 0:N] if b < B // 2 else (po[:, 0, 0:N], pf[:, 1, 0:N])[b % 2]

        def gn_bank(n):
            return po[:, 0, :] if n < 2 else pf[:, 0, :] if n < 6 else ps[:, 1, :]

        FIRST_TURN = HC * MLP_LAG

        def hidden_bank(n):
            return pf[:, 0, :] if n < FIRST_TURN else (pf[:, 0, :], pm[:, 0, :], pm[:, 1, :])[(n - FIRST_TURN) % 3]

        def hidden_before(n):
            return n - 1 if n <= FIRST_TURN else n - 3 if n >= FIRST_TURN + 3 else None

        def acc_bank(i):
            return pf[:, 1, 0:N] if i <= MLP_LAG or i % 2 == 0 else ps[:, 0, 0:N]

        fac_in = sem("fac_in")
        bias_in = sem("bias_in")
        vec_in = sem("vec_in")
        const_in = sem("const_in")
        wqk_in = sem("wqk_in")
        w_in = sem("w_in")
        wmlp_in = sem("wmlp_in")
        win_in = [[sem(f"win_in{t}{h}") for h in range(2)] for t in range(NWIN)]
        kron_ready = sem("kron_ready")
        biased_dve, biased_pool = sem("biased_dve"), sem("biased_pool")
        up_done = sem("up_done")
        neg_ready = sem("neg_ready")
        up_ready = sem("up_ready")
        down_done = sem("down_done")
        y_ready = sem("y_ready")
        bn_raw = sem("bn_raw")
        mean_ready = sem("mean_ready")
        gn_step = sem("gn_step")
        gn_done = sem("gn_done")
        gn_read = sem("gn_read")
        gn_var = sem("gn_var")
        gn_rstd = sem("gn_rstd")
        gn_ready = sem("gn_ready")
        pool_step = sem("pool_step")
        wqk_split = sem("wqk_split")
        wmlp_split = sem("wmlp_split")
        rest_ready = sem("rest_ready")
        warm_ready = sem("warm_ready")
        consts_ready = sem("consts_ready")
        stacks_clear = sem("stacks_clear")
        xn_made = sem("xn_made")
        xn_ready = sem("xn_ready")
        qk_done = sem("qk_done")
        qk_hi = sem("qk_hi")
        qk_lo = sem("qk_lo")
        stack_in = [sem(f"stack_in{r}") for r in range(RING)]
        v_done = sem("v_done")
        v_ready = sem("v_ready")
        max_done = sem("max_done")
        max_read = sem("max_read")
        turn_done = sem("turn_done")
        rows_read = sem("rows_read")
        row_in = sem("row_in")
        scores_done = sem("scores_done")
        probs_ready = sem("probs_ready")
        pv_done = sem("pv_done")
        sums_ready = sem("sums_ready")
        den_done = sem("den_done")
        inv_ready = sem("inv_ready")
        inv_wide_ready = sem("inv_wide_ready")
        inv_done = sem("inv_done")
        weighted_ready = sem("weighted_ready")
        proj_done = sem("proj_done")
        attn_ready = sem("attn_ready")
        xm_made = sem("xm_made")
        xm_ready = sem("xm_ready")
        hidden_done = sem("hidden_done")
        squash_ready = sem("squash_ready")
        swish_ready = sem("swish_ready")
        gated_made = sem("gated_made")
        hi_made = sem("hi_made")
        gated_ready = sem("gated_ready")
        late_gated_ready = sem("late_gated_ready")
        mlp_done = sem("mlp_done")
        result_ready = sem("result_ready")
        stored = sem("stored")

        block = ctx.enter_context(nc.Block())

        @block.sync
        def _(sp):
            sp.dma_start(bias_bc[:, :], bass.AP(tensor=bias0.tensor, offset=0, ap=[[0, 128], [1, C]])).then_inc(bias_in, 16)
            for half in range(2):
                for t in range(NWIN):
                    r0 = WINDOW_ROWS[t] * W
                    sp.dma_start(win_at(t, half), xw[r0:r0 + 128, half * BH:(half + 1) * BH]).then_inc(win_in[t][half], 16)
            sp.dma_start(vec[:, :], vecs).then_inc(vec_in, 16)
            sp.dma_start(ident_s[:, :], ident).then_inc(const_in, 16)
            sp.dma_start(gmat_s[:, :], gmat).then_inc(const_in, 16)
            sp.dma_start(wqk_s[:, :], wqk).then_inc(wqk_in, 16)
            sp.dma_start(wv_s[:, :], wv).then_inc(w_in, 16)
            sp.dma_start(wo_s[:, :, :], wo).then_inc(w_in, 16)
            sp.dma_start(bv_bc[:, :], bass.AP(tensor=bv.tensor, offset=0, ap=[[0, 128], [1, C]])).then_inc(w_in, 16)
            sp.dma_start(w1_s[:, :], w1).then_inc(wmlp_in, 16)
            sp.dma_start(w2_s[:, :], w2).then_inc(wmlp_in, 16)

            def stack(i, k):
                if i < RING:
                    sp.wait_ge(stacks_clear, 2 * (i + 1))
                else:
                    sp.wait_ge(scores_done, HEADS * (i - 2))
                for part, ready, rows in ((0, qk_hi, ((0, 1), (0, 2))), (1, qk_lo, ((2,), (1,)))):
                    for j, s in enumerate((q_stack, k_stack)):
                        sp.wait_ge(ready, 2 * i + j + 1)
                        for r in rows[j]:
                            sp.dma_start(s[k][r * D:(r + 1) * D, :, :].bitcast(F32),
                                         qk_parts[:, i % 2, j, part, :].bitcast(F32)).then_inc(stack_in[k], 16)

            for i in range(B):
                stack(i, i % RING)
            for b in range(B):
                sp.wait_ge(result_ready, b + 1)
                sp.dma_start(out[b], result[:, b * N:(b + 1) * N]).then_inc(stored, 16)
            sp.wait_ge(stored, 16 * B)

        @block.gpsimd
        def _(pool):
            steps = 0

            def split(hi, lo, src):
                nonlocal steps
                pool.tensor_scalar(hi, src, 1.0, 0.0, ALU.mult, ALU.add).then_inc(pool_step, 1)
                steps += 1
                pool.wait_ge(pool_step, steps)
                return pool.tensor_tensor(lo, src, hi.bitcast(F32), ALU.subtract)

            pool.dma_start(fac[:, :], factors).then_inc(fac_in, 16)
            pool.wait_ge(bias_in, 16)

            def add_bias(n):
                t, half = POOL_WINDOWS[n]
                pool.wait_ge(win_in[t][half], 16)
                x4 = win_at(t, half).rearrange("p (b c) -> p b c", c=C)
                pool.tensor_tensor(x4, x4, bias_bc[:, None, :].to_broadcast([128, B // 2, C]), ALU.add).then_inc(biased_pool, 1)

            def rsqrt(n):
                b0, b1 = GN_BATCHES[n]
                pool.wait_ge(gn_var, n + 1)
                pool.tensor_tensor(rstd[:, b0:b1], ve[:, b0:b1], half_neg[:, b0:b1], ALU.pow).then_inc(gn_rstd, 1)

            def normalise(i):
                k = i % RING
                pool.wait_ge(gn_ready, 1 if i == 0 else 2 if i < B // 2 else 3)
                if i >= RING:
                    pool.wait_ge(qk_done, i - RING + 1)
                    pool.wait_ge(v_done, i - RING + 1)
                pool.tensor_scalar(xn[:, k, :], y[:, i, :], scale1[:, i:i + 1], shift1[:, i:i + 1],
                                   ALU.mult, ALU.add).then_inc(xn_made, 1)
                pool.wait_ge(xn_made, 2 * i + 1)
                pool.tensor_scalar(xn_hi[:, k, :], xn[:, k, :], 1.0, 0.0, ALU.mult, ALU.add).then_inc(xn_made, 1)
                pool.wait_ge(xn_made, 2 * i + 2)
                pool.tensor_tensor(xn_lo[:, k, :], xn[:, k, :], xn_hi[:, k, :].bitcast(F32), ALU.subtract).then_inc(xn_ready, 1)

            def rows(i):
                pool.wait_ge(rows_read, i + 1)
                pool.dma_start(q_stack[i % RING][ROW:ROW + 1, :, :].bitcast(F32), max_row[:, :].bitcast(F32)).then_inc(row_in, 16)

            def split_wqk():
                pool.wait_ge(wqk_in, 16)
                split(wqk_hi[:, :], wqk_lo[:, :], wqk_s[:, :]).then_inc(wqk_split, 1)

            def split_w1():
                pool.wait_ge(wmlp_in, 32)
                split(w1_hi[:, :], w1_lo[:, :], w1_s[:, :]).then_inc(wmlp_split, 1)

            def split_w2():
                split(w2_hi[:, :], w2_lo[:, :], w2_s[:, :]).then_inc(wmlp_split, 1)

            def constants():
                pool.memset(half_neg[:, :], -0.5).then_inc(consts_ready, 1)
                pool.memset(v_aug[:, :, :, :, :], 0.0).then_inc(consts_ready, 1)
                pool.wait_ge(consts_ready, 2)
                flat = v_aug[:, :, :, :, :].rearrange("p r c a s -> p (r c) a s")
                for a in range(2):
                    b = D - D * a
                    heads = flat[:, :, a, b:b + HALF * 32].rearrange("p n (g s) -> p n g s", s=32)
                    pool.memset(heads[:, :, :, D - D * a], 1.0).then_inc(consts_ready, 1)
                    if a == 0:
                        pool.wait_ge(consts_ready, 3)

            def second_norm(i):
                cols = slice(i * N, (i + 1) * N)
                pool.wait_ge(gn_ready, [n for n, (_, end) in enumerate(GN_BATCHES) if n >= len(GN1_BATCHES) and i < end][0] + 1)
                pool.tensor_scalar(xm[:, cols], attn[:, i, :], scale2[:, i:i + 1], shift2[:, i:i + 1],
                                   ALU.mult, ALU.add).then_inc(xm_made, 1)
                pool.tensor_scalar(xm_hi[:, cols], attn[:, i, :], scale2[:, i:i + 1], shift2[:, i:i + 1],
                                   ALU.mult, ALU.add).then_inc(xm_made, 1)
                pool.wait_ge(xm_made, 2 * i + 2)
                pool.tensor_tensor(xm_lo[:, cols], xm[:, cols], xm_hi[:, cols].bitcast(F32), ALU.subtract).then_inc(xm_ready, 1)

            def gated_low(n):
                pool.wait_ge(hi_made, n + 1)
                pool.tensor_tensor(gated_lo[:, n % MLP_RING, :], gated[:, n % MLP_RING, :],
                                   gated_hi[:, n % MLP_RING, :].bitcast(F32), ALU.subtract).then_inc(gated_ready, 1)

            constants()
            for n in range(6):
                add_bias(n)
            split_wqk()
            rsqrt(0)
            add_bias(6)
            normalise(0)
            add_bias(7)
            rsqrt(1)
            normalise(1)
            split_w1()
            normalise(2)
            rows(0)
            for i in range(B):
                nxt, n = i + 1 < B, HC * (i - MLP_LAG)
                if i == 0:
                    rsqrt(2)
                if n >= 0:
                    gated_low(n)
                    gated_low(n + 1)
                if i in (3, 5, 7):
                    rsqrt(3 + (i - 3) // 2)
                if i + RING < B:
                    normalise(i + RING)
                if i == 1:
                    split_w2()
                if n >= 0:
                    gated_low(n + 2)
                if i in (3, 5, 7):
                    second_norm(i - 3)
                if nxt:
                    rows(i + 1)
                if n >= 0:
                    gated_low(n + 3)
                if i in (3, 5, 7):
                    second_norm(i - 2)
            rsqrt(6)
            second_norm(6)
            rsqrt(7)
            second_norm(7)

        @block.scalar
        def _(act):
            def fill(stack, column):
                act.activation(stack[:, :, :].rearrange("p h n -> p (h n)"),
                               rest[:, column:column + 1].to_broadcast([128, HEADS * N]), ACT.Copy).then_inc(stacks_clear, 1)

            def negative(n):
                act.wait_ge(up_done, n + 1)
                if n >= 2:
                    act.wait_ge(up_ready, n - 1)
                act.activation(lrelu_neg[:, n % 2, :], up_bank[n % 4], ACT.Copy,
                               scale=SLOPE * GAIN * UPGAIN).then_inc(neg_ready, 1)

            def read_y(b):
                act.wait_ge(down_done, b + 1)
                act.activation(y[:, b, :], down_bank(b), ACT.Copy).then_inc(y_ready, 1)

            def high_parts(i):
                act.wait_ge(vec_in, 16)
                act.wait_ge(qk_done, i + 1)
                if i >= 2:
                    act.wait_ge(stack_in[(i - 2) % RING], 32 * STACKED * ((i - 2) // RING + 1))
                act.activation(qk_parts[:, i % 2, 0, 0, :], px[:, 0, 0:N], ACT.Identity, bias=bq).then_inc(qk_hi, 1)
                act.activation(qk_parts[:, i % 2, 1, 0, :], px[:, 0, N:2 * N], ACT.Identity, bias=bk).then_inc(qk_hi, 1)

            def exponentials(i, h):
                act.wait_ge(scores_done, HEADS * i + h + 1)
                if i:
                    act.wait_ge(pv_done, 2 * (i - 1) + h // HALF + 1)
                act.activation(probs[:, h // HALF, h % HALF, :, :].rearrange("p c n -> p (c n)"),
                               ps[:, h % 2, :], ACT.Exp, scale=D ** -0.5).then_inc(probs_ready, 1)

            def read_sums(i):
                act.wait_ge(pv_done, 2 * (i + 1))
                if i:
                    act.wait_ge(weighted_ready, i)
                act.activation(sums[:, :, :].rearrange("p a n -> p (a n)"), po[:, 0, :], ACT.Copy).then_inc(sums_ready, 1)

            def spread_inverse(i):
                act.wait_ge(inv_ready, i + 1)
                if i:
                    act.wait_ge(inv_done, i)
                act.activation(inv_wide[:, :, :].rearrange("p c (h d) -> p (c h) d", d=D),
                               inv[:, :, :, :].rearrange("p c g a -> p (c g a)")[:, :, None].to_broadcast([128, 2 * HEADS, D]),
                               ACT.Copy).then_inc(inv_wide_ready, 1)

            def read_proj(i):
                act.wait_ge(proj_done, i + 1)
                dst = attn[:, i, :] if isinstance(i, int) else attn[:, bass.ds(i, 1), :].rearrange("p a n -> p (a n)")
                act.activation(dst, px[:, 0, 0:N], ACT.Identity, bias=bo).then_inc(attn_ready, 1)

            def read_rows(i):
                act.wait_ge(turn_done, i + 1)
                if i:
                    act.wait_ge(row_in, 16 * i)
                act.activation(max_row[:, :], pm[0:HEADS, 1, 0:N], ACT.Copy).then_inc(rows_read, 1)

            def squash(n):
                act.wait_ge(hidden_done, n + 1)
                if n >= MLP_RING:
                    act.wait_ge(gated_made, n - MLP_RING + 1)
                src, dst = hidden_bank(n)[:, 0:N], squashed[:, n % MLP_RING, :]
                if n < FIRST_TURN:
                    act.activation(dst, src, ACT.Tanh, scale=0.5).then_inc(squash_ready, 1)
                else:
                    act.activation(dst, src, ACT.Silu).then_inc(squash_ready, 1)

            def gated_high(n):
                act.wait_ge(gated_made, n + 1)
                if n >= MLP_RING:
                    act.wait_ge(mlp_done, n - MLP_RING + 1)
                act.activation(gated_hi[:, n % MLP_RING, :], gated[:, n % MLP_RING, :], ACT.Copy).then_inc(hi_made, 1)

            act.wait_ge(rest_ready, 2)
            fills = [(s[r], c) for r in range(RING) for s, c in ((q_stack, 1), (k_stack, 0))]
            fill(*fills[0])
            for n in range(8):
                negative(n)
            fill(*fills[1])
            read_y(0)
            fill(*fills[2])
            negative(8)
            read_y(1)
            negative(9)
            fill(*fills[3])
            read_y(2)
            negative(10)
            read_y(3)
            high_parts(0)
            for n in range(11, 16):
                negative(n)
            read_y(4)
            high_parts(1)
            read_y(5)
            fill(*fills[4])
            fill(*fills[5])
            read_y(6)
            read_y(7)
            read_rows(0)
            for i in range(B):
                nxt, prev, n = i + 1 < B, i >= 1, HC * (i - MLP_LAG)
                if i >= 2:
                    read_proj(i - 2)
                if n >= 0:
                    squash(n)
                if i + 2 < B:
                    high_parts(i + 2)
                if prev:
                    read_sums(i - 1)
                if n >= 0:
                    gated_high(n)
                exponentials(i, 0)
                if n >= 0:
                    squash(n + 1)
                exponentials(i, 1)
                exponentials(i, 2)
                exponentials(i, 3)
                if n >= 0:
                    gated_high(n + 1)
                    squash(n + 2)
                if prev:
                    spread_inverse(i - 1)
                exponentials(i, 4)
                if n >= 0:
                    gated_high(n + 2)
                exponentials(i, 5)
                if n >= 0:
                    squash(n + 3)
                if nxt:
                    read_rows(i + 1)
                exponentials(i, 6)
                exponentials(i, 7)
                if n >= 0:
                    gated_high(n + 3)
            read_proj(B - 2)
            squash(16)
            squash(17)
            read_sums(B - 1)
            squash(18)
            gated_high(16)
            gated_high(17)
            squash(19)
            spread_inverse(B - 1)
            gated_high(18)
            gated_high(19)
            squash(20)
            squash(21)
            read_proj(B - 1)
            squash(22)
            squash(23)
            gated_high(20)
            squash(24)
            gated_high(21)
            squash(25)
            gated_high(22)
            gated_high(23)
            squash(26)
            squash(27)
            gated_high(24)
            gated_high(25)
            squash(28)
            gated_high(26)
            gated_high(27)
            squash(29)
            gated_high(28)
            squash(30)
            squash(31)
            for n in range(29, 32):
                gated_high(n)

        @block.tensor
        def _(pe):
            def three(dst, w_hi, w_lo, x_hi, x_lo, start, stop):
                pe.matmul(dst, w_hi, x_hi, start=start, stop=False)
                pe.matmul(dst, w_hi, x_lo, start=False, stop=False)
                return pe.matmul(dst, w_lo, x_hi, start=False, stop=stop)

            def upsample(n):
                half, m = divmod(n, CHUNKS)
                window = (WINDOW_OF[m], half)
                if window in DVE_WINDOWS:
                    pe.wait_ge(biased_dve, DVE_WINDOWS.index(window) + 1)
                else:
                    pe.wait_ge(biased_pool, POOL_WINDOWS.index(window) + 1)
                pe.wait_ge(kron_ready, UP_WEIGHT_OF[m] + 1)
                if n >= 4:
                    pe.wait_ge(up_ready, n - 3)
                pe.matmul(up_bank[n % 4], up_w[:, UP_WEIGHT_OF[m], :, :].rearrange("p a b -> p (a b)"),
                          win_at(WINDOW_OF[m], half), start=True, stop=True).then_inc(up_done, 1)

            def group_means(n):
                b0, b1 = GN_BATCHES[n]
                if n < 2:
                    pe.wait_ge(const_in, 32)
                if n == 1:
                    pe.wait_ge(gn_read, 1)
                if n in (4, 5):
                    pe.wait_ge(gated_made, 2 * HC * (n - 4) + HC + 2)
                if n >= 6:
                    pe.wait_ge(probs_ready, HEADS * B)
                pe.wait_ge(mean_ready, n + 1)
                pe.matmul(gn_bank(n)[:, 0:2 * (b1 - b0)], gmat_s[:, :], mv[:, b0:b1, :].rearrange("p b s -> p (b s)"),
                          start=True, stop=True).then_inc(gn_done, 1)

            def downsample(b):
                half = b // (B // 2)
                if b == 0:
                    pe.wait_ge(kron_ready, UP_VARIANTS + 1)
                if b == 4:
                    pe.wait_ge(gn_read, 2)
                if b in (2, 3, 6, 7):
                    pe.wait_ge(y_ready, b - 1)
                col = (b % (B // 2)) * C
                for m in range(CHUNKS):
                    pe.wait_ge(up_ready, CHUNKS * half + m + 1)
                    o0, o1 = max(0, 2 * m - 3), min(W, 2 * m + 5)
                    mm = pe.matmul(down_bank(b)[:, o0 * W:o1 * W], up_at(m, half)[:, col:col + C],
                                   dn_w[:, o0 - 2 * m + 3:o1 - 2 * m + 3, :].rearrange("p a b -> p (a b)"),
                                   start=(m == 0), stop=(m == CHUNKS - 1), skip_group_check=True)
                mm.then_inc(down_done, 1)

            def project_qk(i):
                pe.wait_ge(wqk_split, 1)
                pe.wait_ge(xn_ready, i + 1)
                if i:
                    pe.wait_ge(v_ready, i)
                if i >= 4:
                    pe.wait_ge(attn_ready, i - 3)
                for j in range(2):
                    mm = three(px[:, 0, j * N:(j + 1) * N], wqk_hi[:, j * C:(j + 1) * C], wqk_lo[:, j * C:(j + 1) * C],
                               xn_hi[:, i % RING, :], xn_lo[:, i % RING, :], True, True)
                mm.then_inc(qk_done, 1)

            def project_v(i):
                pe.wait_ge(w_in, 48)
                pe.wait_ge(qk_lo, 2 * (i + 1))
                for c in range(2):
                    mm = pe.matmul(px[:, 0, c * C:(c + 1) * C], xn[:, i % RING, c * 128:(c + 1) * 128], wv_s[:, :],
                                   start=True, stop=True)
                mm.then_inc(v_done, 1)

            def maxima(i, h):
                k = i % RING
                if h == 0:
                    pe.wait_ge(stack_in[k], 32 * STACKED * (i // RING + 1))
                    if i == 0:
                        pe.wait_ge(y_ready, B // 2)
                if h == 1 and i:
                    pe.wait_ge(rows_read, i)
                elif HEADS * i + h >= 2:
                    pe.wait_ge(max_read, HEADS * i + h - 1)
                for c in range(2):
                    mm = pe.matmul(pm[:, h % 2, c * N:(c + 1) * N], q_stack[k][:, h, c * 128:(c + 1) * 128],
                                   k_stack[k][:, h, :], start=True, stop=True)
                mm.then_inc(max_done, 1)

            def turn_maxima(i):
                pe.wait_ge(max_read, HEADS * (i + 1))
                for c in range(2):
                    mm = pe.transpose(pm[0:HEADS, 1, c * 128:(c + 1) * 128], neg_max[:, c, :], ident_s[:, :])
                mm.then_inc(turn_done, 1)

            def scores(i, h):
                if h == 0:
                    pe.wait_ge(row_in, 16 * (i + 1))
                if HEADS * i + h >= 2:
                    pe.wait_ge(probs_ready, HEADS * i + h - 1)
                for c in range(2):
                    mm = pe.matmul(ps[:, h % 2, c * N:(c + 1) * N], k_stack[i % RING][:, h, c * 128:(c + 1) * 128],
                                   q_stack[i % RING][:, h, :], start=True, stop=True)
                mm.then_inc(scores_done, 1)

            def weigh(i, half, c):
                if c == 0:
                    pe.wait_ge(probs_ready, HEADS * i + HALF * (half + 1))
                    pe.wait_ge(v_ready, i + 1)
                    if half == 0 and i:
                        pe.wait_ge(sums_ready, i)
                    elif half == 0:
                        pe.wait_ge(y_ready, B)
                b = D - D * half
                for g in range(HALF):
                    mm = pe.matmul(po[32 * g:32 * g + 32, 0, half * N:(half + 1) * N],
                                   v_aug[:, i % RING, c, half, b + 32 * g:b + 32 * g + 32], probs[:, half, g, c, :],
                                   start=(c == 0), stop=(c == 1), skip_group_check=True)
                if c == 1:
                    mm.then_inc(pv_done, 1)

            def turn_sums(i):
                pe.wait_ge(sums_ready, i + 1)
                if i + 3 < B:
                    pe.wait_ge(v_ready, i + 4)
                elif i:
                    pe.wait_ge(attn_ready, i)
                for c in range(2):
                    for half in range(2):
                        a = (2 * c + half) * 128
                        mm = pe.transpose(px[:, 0, a:a + 128], sums[:, half, c * 128:(c + 1) * 128], ident_s[:, :])
                mm.then_inc(den_done, 1)

            def turn_inverse(i):
                pe.wait_ge(inv_wide_ready, i + 1)
                for c in range(2):
                    mm = pe.transpose(px[:, 0, c * 128:(c + 1) * 128], inv_wide[:, c, :], ident_s[:, :])
                mm.then_inc(inv_done, 1)

            def project_out(i):
                pe.wait_ge(weighted_ready, i + 1)
                for half in range(2):
                    mm = pe.matmul(px[:, 0, 0:N], wo_s[:, half, :], weighted[:, half, :], start=(half == 0), stop=(half == 1))
                mm.then_inc(proj_done, 1)

            def hidden(n):
                i, hc = divmod(n, HC)
                if hc == 0:
                    pe.wait_ge(wmlp_split, 1)
                    pe.wait_ge(xm_ready, i + 1)
                if n in (HC + 2, 3 * HC + 2):
                    pe.wait_ge(gn_read, 5 + n // (2 * HC))
                before = hidden_before(n)
                if before is None:
                    pe.wait_ge(rows_read, B)
                elif before >= 0:
                    pe.wait_ge(gated_made, before + 1)
                cols = slice(i * N, (i + 1) * N)
                for j in range(2):
                    a = j * HIDDEN + hc * C
                    mm = three(hidden_bank(n)[:, j * N:(j + 1) * N], w1_hi[:, a:a + C], w1_lo[:, a:a + C],
                               xm_hi[:, cols], xm_lo[:, cols], True, True)
                mm.then_inc(hidden_done, 1)

            def down_project(n):
                i, hc = divmod(n, HC)
                if n < FIRST_TURN:
                    pe.wait_ge(gated_ready, n + 1)
                else:
                    pe.wait_ge(late_gated_ready, n - FIRST_TURN + 1)
                if hc == 0:
                    pe.wait_ge(wmlp_split, 2)
                    if i == MLP_LAG + 1:
                        pe.wait_ge(probs_ready, HEADS * B)
                    elif i:
                        pe.wait_ge(result_ready, i if i <= MLP_LAG else i - 1)
                three(acc_bank(i), w2_hi[:, hc * C:(hc + 1) * C], w2_lo[:, hc * C:(hc + 1) * C],
                      gated_hi[:, n % MLP_RING, :], gated_lo[:, n % MLP_RING, :], hc == 0, hc == HC - 1).then_inc(mlp_done, 1)

            pe.wait_ge(warm_ready, 1)
            for _ in range(WARM_UP):
                pe.matmul(px[:, 0, 0:N], y[:, 0, 0:128], y[:, 0, :], start=True, stop=True)

            for n in range(8):
                upsample(n)
            downsample(0)
            downsample(1)
            upsample(8)
            group_means(0)
            upsample(9)
            downsample(2)
            upsample(10)
            downsample(3)
            project_qk(0)
            upsample(11)
            upsample(12)
            group_means(1)
            for n in range(13, 16):
                upsample(n)
            project_v(0)
            downsample(4)
            maxima(0, 0)
            downsample(5)
            maxima(0, 1)
            maxima(0, 2)
            project_qk(1)
            maxima(0, 3)
            downsample(6)
            maxima(0, 4)
            maxima(0, 5)
            maxima(0, 6)
            project_v(1)
            maxima(0, 7)
            downsample(7)
            turn_maxima(0)

            for i in range(B):
                nxt, prev, qkv, n = i + 1 < B, i >= 1, i + 2 < B, HC * (i - MLP_LAG)
                if nxt:
                    maxima(i + 1, 0)
                    maxima(i + 1, 1)
                if n >= 0:
                    hidden(n)
                if qkv:
                    project_qk(i + 2)
                if nxt:
                    maxima(i + 1, 2)
                if prev:
                    weigh(i - 1, 1, 0)
                    weigh(i - 1, 1, 1)
                if n >= 1:
                    down_project(n - 1)
                if nxt:
                    maxima(i + 1, 3)
                scores(i, 0)
                if n >= 0:
                    hidden(n + 1)
                scores(i, 1)
                if i == 0:
                    group_means(2)
                if nxt:
                    maxima(i + 1, 4)
                if qkv:
                    project_v(i + 2)
                scores(i, 2)
                if nxt:
                    maxima(i + 1, 5)
                if n >= 0:
                    down_project(n)
                scores(i, 3)
                if i in (3, 5, 7):
                    group_means(3 + (i - 3) // 2)
                if prev:
                    turn_sums(i - 1)
                scores(i, 4)
                if n >= 0:
                    hidden(n + 2)
                if nxt:
                    maxima(i + 1, 6)
                weigh(i, 0, 0)
                if nxt:
                    maxima(i + 1, 7)
                scores(i, 5)
                if n >= 0:
                    down_project(n + 1)
                if prev:
                    turn_inverse(i - 1)
                weigh(i, 0, 1)
                if n >= 0:
                    hidden(n + 3)
                if nxt:
                    turn_maxima(i + 1)
                scores(i, 6)
                scores(i, 7)
                if n >= 0:
                    down_project(n + 2)
                if prev:
                    project_out(i - 1)

            weigh(B - 1, 1, 0)
            weigh(B - 1, 1, 1)
            hidden(16)
            group_means(6)
            for n in range(17, 20):
                hidden(n)
            turn_sums(B - 1)
            down_project(15)
            hidden(20)
            turn_inverse(B - 1)
            hidden(21)
            down_project(16)
            project_out(B - 1)
            down_project(17)
            hidden(22)
            hidden(23)
            group_means(7)
            hidden(24)
            down_project(18)
            hidden(25)
            down_project(19)
            hidden(26)
            down_project(20)
            hidden(27)
            for n in range(21, 24):
                down_project(n)
            hidden(28)
            hidden(29)
            down_project(24)
            hidden(30)
            hidden(31)
            for n in range(25, 32):
                down_project(n)

        @block.vector
        def _(dve):
            steps = 0

            def chain(ins):
                nonlocal steps
                steps += 1
                ins.then_inc(gn_step, 1)
                dve.wait_ge(gn_step, steps)

            dve.memset(y[:, 0, :], 0.0).then_inc(warm_ready, 1)
            dve.memset(rest[:, :], 0.0).then_inc(rest_ready, 1)
            dve.wait_ge(rest_ready, 1)
            dve.memset(rest[ROW:ROW + 1, 0:1], 1.0).then_inc(rest_ready, 1)
            fast = fac[:, 0:32]
            slow = fac[:, 32:52].rearrange("p (v a) -> p v a", v=UP_VARIANTS)
            dve.wait_ge(fac_in, 16)
            dve.wait_ge(bias_in, 16)

            def up_weights(v):
                dve.tensor_tensor(up_w[:, v, :, :], slow[:, v, :, None].to_broadcast([128, 4, 32]),
                                  fast[:, None, :].to_broadcast([128, 4, 32]), ALU.mult).then_inc(kron_ready, 1)

            def down_weights():
                dve.tensor_tensor(dn_w[:, :, :], fac[:, 68:76, None].to_broadcast([128, 8, 16]),
                                  fac[:, None, 52:68].to_broadcast([128, 8, 16]), ALU.mult).then_inc(kron_ready, 1)

            def add_bias(n):
                t, half = DVE_WINDOWS[n]
                dve.wait_ge(win_in[t][half], 16)
                x4 = win_at(t, half).rearrange("p (b c) -> p b c", c=C)
                dve.tensor_tensor(x4, x4, bias_bc[:, None, :].to_broadcast([128, B // 2, C]), ALU.add).then_inc(biased_dve, 1)

            def leaky(n):
                dve.wait_ge(neg_ready, n + 1)
                dve.scalar_tensor_tensor(out=up_at(n % CHUNKS, n // CHUNKS), in0=up_bank[n % 4], scalar=GAIN * UPGAIN,
                                         in1=lrelu_neg[:, n % 2, :], op0=ALU.mult, op1=ALU.max).then_inc(up_ready, 1)

            def means(n):
                s = slice(*GN_BATCHES[n])
                if n >= len(GN1_BATCHES):
                    dve.wait_ge(bn_raw, 2 * GN_BATCHES[n][1])
                chain(dve.tensor_tensor(sq[:, s], mv[:, s, 0], mv[:, s, 0], ALU.mult))
                dve.tensor_tensor(mv[:, s, 1], mv[:, s, 1], sq[:, s], ALU.add).then_inc(mean_ready, 1)

            def variance(n):
                b0, b1 = GN_BATCHES[n]
                s = slice(b0, b1)
                dve.wait_ge(gn_done, n + 1)
                dve.tensor_copy(gs[:, s, :], gn_bank(n)[:, 0:2 * (b1 - b0)].rearrange("p (b s) -> p b s", s=2)).then_inc(gn_read, 1)
                dve.wait_ge(gn_read, n + 1)
                chain(dve.tensor_tensor(sq[:, s], gs[:, s, 0], gs[:, s, 0], ALU.mult))
                chain(dve.tensor_tensor(sq[:, s], gs[:, s, 1], sq[:, s], ALU.subtract))
                dve.tensor_scalar(ve[:, s], sq[:, s], EPS, None, ALU.add).then_inc(gn_var, 1)

            def coefficients(n):
                s = slice(*GN_BATCHES[n])
                if n < len(GN1_BATCHES):
                    gamma, beta, scale, shift = g1w, g1b, scale1, shift1
                else:
                    gamma, beta, scale, shift = g2w, g2b, scale2, shift2
                dve.wait_ge(vec_in, 16)
                dve.wait_ge(gn_rstd, n + 1)
                chain(dve.tensor_scalar(scale[:, s], rstd[:, s], gamma, None, ALU.mult))
                chain(dve.tensor_tensor(shift_t[:, s], gs[:, s, 0], scale[:, s], ALU.mult))
                dve.tensor_scalar(shift[:, s], shift_t[:, s], -1.0, beta, ALU.mult, ALU.add).then_inc(gn_ready, 1)

            def y_statistics(b):
                dve.wait_ge(y_ready, b + 1)
                chain(dve.bn_stats(stat6[:, b, :], y[:, b, :]))
                chain(dve.bn_aggr(mv[:, b, :], stat6[:, b, :]))

            def low_parts(i):
                dve.wait_ge(qk_hi, 2 * (i + 1))
                for j, bias in enumerate((bq, bk)):
                    dve.scalar_tensor_tensor(out=qk_parts[:, i % 2, j, 1, :], in0=px[:, 0, j * N:(j + 1) * N], scalar=bias,
                                             in1=qk_parts[:, i % 2, j, 0, :].bitcast(F32), op0=ALU.add,
                                             op1=ALU.subtract).then_inc(qk_lo, 1)

            def read_v(i):
                dve.wait_ge(v_done, i + 1)
                dve.wait_ge(w_in, 48)
                dve.wait_ge(consts_ready, 4)
                if i >= RING:
                    dve.wait_ge(pv_done, 2 * (i - 2))
                heads = v_aug[:, i % RING, :, :, D:].rearrange("p c a (g s) -> p c a g s", s=32)[:, :, :, :, 0:D]
                dve.tensor_tensor(heads, px[:, 0, 0:2 * C].rearrange("p (c a g d) -> p c a g d", c=2, a=2, d=D),
                                  bv_bc[:, :].rearrange("p (a g d) -> p a g d", a=2, d=D)[:, None, :, :, :].to_broadcast([128, 2, 2, HALF, D]),
                                  ALU.add).then_inc(v_ready, 1)

            def reduce_max(i, h):
                dve.wait_ge(max_done, HEADS * i + h + 1)
                if h == 0 and i:
                    dve.wait_ge(turn_done, i)
                dve.tensor_reduce(neg_max[:, :, h], pm[:, h % 2, :].rearrange("p (c n) -> p c n", c=2),
                                  AX.X, ALU.max, negate=True).then_inc(max_read, 1)

            def invert(i):
                dve.wait_ge(den_done, i + 1)
                if i:
                    dve.wait_ge(inv_wide_ready, i)
                turned = px[:, 0, :].rearrange("p (c a g s) -> p c a g s", c=2, a=2, s=32)
                for a in range(2):
                    ins = dve.reciprocal(inv[:, :, :, a], turned[:, :, a, :, D - D * a])
                ins.then_inc(inv_ready, 1)

            def normalise(i):
                dve.wait_ge(inv_done, i + 1)
                if i:
                    dve.wait_ge(proj_done, i)
                dve.tensor_tensor(weighted[:, :, :], px[:, 0, None, 0:N].to_broadcast([128, 2, N]), sums[:, :, :],
                                  ALU.mult).then_inc(weighted_ready, 1)

            def statistics(i):
                ii = slice(i, i + 1) if isinstance(i, int) else bass.ds(i, 1)
                dve.wait_ge(attn_ready, i + 1)
                dve.bn_stats(stat6[:, ii, :].rearrange("p a s -> p (a s)"), attn[:, ii, :].rearrange("p a n -> p (a n)")).then_inc(bn_raw, 1)
                dve.wait_ge(bn_raw, 2 * i + 1)
                dve.bn_aggr(mv[:, ii, :].rearrange("p a s -> p (a s)"), stat6[:, ii, :].rearrange("p a s -> p (a s)")).then_inc(bn_raw, 1)

            def gate(n):
                dve.wait_ge(squash_ready, n + 1)
                if n >= FIRST_TURN:
                    if n < FIRST_TURN + MLP_RING:
                        dve.wait_ge(gated_ready, n - MLP_RING + 1)
                    else:
                        dve.wait_ge(late_gated_ready, n - MLP_RING - FIRST_TURN + 1)
                    dve.tensor_tensor(gated[:, n % MLP_RING, :], squashed[:, n % MLP_RING, :], hidden_bank(n)[:, N:2 * N],
                                      ALU.mult).then_inc(gated_made, 1)
                    return
                dve.scalar_tensor_tensor(out=swish[:, n % MLP_RING, :], in0=squashed[:, n % MLP_RING, :], scalar=1.0,
                                         in1=hidden_bank(n)[:, 0:N], op0=ALU.add, op1=ALU.mult).then_inc(swish_ready, 1)
                dve.wait_ge(swish_ready, n + 1)
                if n >= MLP_RING:
                    dve.wait_ge(gated_ready, n - MLP_RING + 1)
                dve.scalar_tensor_tensor(out=gated[:, n % MLP_RING, :], in0=swish[:, n % MLP_RING, :], scalar=0.5,
                                         in1=hidden_bank(n)[:, N:2 * N], op0=ALU.mult, op1=ALU.mult).then_inc(gated_made, 1)

            def gated_low(n):
                dve.wait_ge(hi_made, n + 1)
                dve.tensor_tensor(gated_lo[:, n % MLP_RING, :], gated[:, n % MLP_RING, :],
                                  gated_hi[:, n % MLP_RING, :].bitcast(F32), ALU.subtract).then_inc(late_gated_ready, 1)

            def residual(i):
                dve.wait_ge(mlp_done, HC * (i + 1))
                dve.tensor_tensor(result[:, i * N:(i + 1) * N], acc_bank(i), y[:, i, :], ALU.add).then_inc(result_ready, 1)

            up_weights(0)
            add_bias(0)
            up_weights(1)
            add_bias(1)
            up_weights(2)
            up_weights(3)
            add_bias(2)
            leaky(0)
            leaky(1)
            up_weights(4)
            add_bias(3)
            down_weights()
            for n in range(2, 8):
                leaky(n)
            y_statistics(0)
            means(0)
            variance(0)
            leaky(8)
            coefficients(0)
            y_statistics(1)
            y_statistics(2)
            leaky(9)
            leaky(10)
            y_statistics(3)
            means(1)
            low_parts(0)
            leaky(11)
            leaky(12)
            variance(1)
            for n in range(13, 16):
                leaky(n)
            coefficients(1)
            read_v(0)
            y_statistics(4)
            reduce_max(0, 0)
            reduce_max(0, 1)
            reduce_max(0, 2)
            low_parts(1)
            reduce_max(0, 3)
            reduce_max(0, 4)
            reduce_max(0, 5)
            y_statistics(5)
            reduce_max(0, 6)
            reduce_max(0, 7)
            read_v(1)
            y_statistics(6)
            y_statistics(7)
            means(2)
            for i in range(B):
                nxt, prev, qkv, n = i + 1 < B, i >= 1, i + 2 < B, HC * (i - MLP_LAG)
                batch = 3 + (i - 3) // 2
                if nxt:
                    reduce_max(i + 1, 0)
                    reduce_max(i + 1, 1)
                if i >= 2:
                    statistics(i - 2)
                if n >= 0:
                    gate(n)
                if nxt:
                    reduce_max(i + 1, 2)
                if qkv:
                    low_parts(i + 2)
                if nxt:
                    reduce_max(i + 1, 3)
                if n >= 1:
                    residual(i - MLP_LAG - 1)
                if i == 0:
                    variance(2)
                if i in (3, 5, 7):
                    means(batch)
                if qkv:
                    read_v(i + 2)
                if n >= 0:
                    gate(n + 1)
                if nxt:
                    reduce_max(i + 1, 4)
                if i in (3, 5, 7):
                    variance(batch)
                if nxt:
                    reduce_max(i + 1, 5)
                if prev:
                    invert(i - 1)
                if nxt:
                    reduce_max(i + 1, 6)
                if n >= 0:
                    gate(n + 2)
                if nxt:
                    reduce_max(i + 1, 7)
                if i in (3, 5, 7):
                    coefficients(batch)
                if i == 0:
                    coefficients(2)
                if prev:
                    normalise(i - 1)
                if n >= 0:
                    gate(n + 3)
            statistics(B - 2)
            means(6)
            gate(16)
            gate(17)
            variance(6)
            gate(18)
            invert(B - 1)
            residual(B - MLP_LAG - 1)
            gate(19)
            gated_low(16)
            normalise(B - 1)
            coefficients(6)
            gated_low(17)
            gate(20)
            gate(21)
            gated_low(18)
            statistics(B - 1)
            means(7)
            gate(22)
            gated_low(19)
            variance(7)
            gate(23)
            gated_low(20)
            coefficients(7)
            gate(24)
            for n in range(21, 24):
                gated_low(n)
            gate(25)
            residual(4)
            gate(26)
            gated_low(24)
            residual(5)
            gate(27)
            gated_low(25)
            gate(28)
            gated_low(26)
            gated_low(27)
            gate(29)
            gated_low(28)
            gate(30)
            gate(31)
            for n in range(29, 32):
                gated_low(n)
            residual(6)
            residual(B - 1)


def kernel(x, L0_conv_bias, L0_conv_up_filter, L0_conv_down_filter, L1_conv_gn1_gamma, L1_conv_gn1_beta,
           L1_conv_qkv_w, L1_conv_qkv_b, L1_conv_out_w, L1_conv_out_b, L1_conv_gn2_gamma, L1_conv_gn2_beta,
           L1_conv_mlp1_w, L1_conv_mlp2_w):
    import numpy as np
    import concourse.bacc as bacc
    from concourse.bass_utils import run_bass_kernel_spmd

    a = np.asarray

    def shifted(filt, rows, cols, tap):
        filt = a(filt)
        table = np.zeros((rows, cols), filt.dtype)
        for j in range(rows):
            for i in range(cols):
                if 0 <= tap(i, j) < filt.shape[0]:
                    table[j, i] = filt[tap(i, j)]
        return table

    up, down = L0_conv_up_filter, L0_conv_down_filter
    up_fast = np.tile(shifted(up, 16, 32, lambda i, j: 5 + i - 2 * j), (8, 1))
    slow = [shifted(up, 8, 4, lambda i, j, s=s: s + i - 2 * j) for s in (5, 9, 11, 13, 17)]
    up_slow = np.repeat(np.concatenate(slow, axis=1), 16, axis=0)
    dn_fast = np.tile(shifted(down, 32, 16, lambda o, r: 6 + 2 * o - r), (4, 1))
    dn_slow = np.repeat(shifted(down, 4, 8, lambda o, r: 2 * o - r), 32, axis=0)

    order = np.arange(C).reshape(HEADS, D).T.ravel()
    w, b = a(L1_conv_qkv_w), a(L1_conv_qkv_b)
    wqk = np.concatenate([w[0:C][order], w[C:2 * C][order]], axis=0).T
    wo = np.zeros((128, 2, C), w.dtype)
    for h in range(HEADS):
        row = 32 * (h % HALF) + D * (h // HALF)
        wo[row:row + D, h // HALF, :] = a(L1_conv_out_w)[:, h * D:(h + 1) * D].T
    vecs = np.zeros((128, 8), w.dtype)
    for j, v in enumerate((L1_conv_gn1_gamma, L1_conv_gn1_beta, L1_conv_gn2_gamma, L1_conv_gn2_beta,
                           b[0:C][order], b[C:2 * C][order], L1_conv_out_b)):
        vecs[:, j] = a(v)
    arrays = {
        "xw": a(x).transpose(2, 3, 0, 1).reshape(N, B * C),
        "factors": np.concatenate([up_fast, up_slow, dn_fast, dn_slow], axis=1),
        "bias0": a(L0_conv_bias), "vecs": vecs, "wqk": wqk, "wv": w[2 * C:].T, "bv": b[2 * C:],
        "wo": wo, "w1": a(L1_conv_mlp1_w).T,
        "w2": a(L1_conv_mlp2_w).T.reshape(HC, C, C).transpose(1, 0, 2).reshape(C, HC * C),
        "ident": np.eye(128, dtype=np.float32),
        "gmat": np.kron(np.eye(32, dtype=np.float32), np.full((4, 4), 0.25, np.float32)),
    }
    arrays = {f"in_{k}": np.ascontiguousarray(v) for k, v in arrays.items()}
    nc = bacc.Bacc("TRN2", target_bir_lowering=False, num_devices=1)
    ins = [nc.dram_tensor(k, v.shape, mybir.dt.from_np(v.dtype), kind="ExternalInput").ap() for k, v in arrays.items()]
    out = nc.dram_tensor("out", (B, C, N), F32, kind="ExternalOutput").ap()
    build(nc, *ins, out)
    r = run_bass_kernel_spmd(nc, [arrays], core_ids=[0])
    return r.results[0]["out"].reshape(B, C, W, W)
```
